# Optimizing a Trainium2 kernel written in Bass

```python
import numpy as np
import jax
import jax.numpy as jnp

def _softmax(x, axis=-1):
    return jax.nn.softmax(x, axis=axis)

def _gelu(x):
    return jax.nn.gelu(x, approximate=True)

def _silu(x):
    return jax.nn.silu(x)

def _sigmoid(x):
    return jax.nn.sigmoid(x)

def _layernorm(x, axis=-1, eps=1e-05):
    m = jnp.mean(x, axis=axis, keepdims=True)
    v = jnp.var(x, axis=axis, keepdims=True)
    return (x - m) / jnp.sqrt(v + eps)

def _scatter_add(tgt, idx, src, axis=0):
    return tgt.at[idx].add(src)

def _segment_sum(src, seg, n):
    return jax.ops.segment_sum(src, seg, n)
kernel_name = 'mk_seq_postln_d2_jaxref_r8_168c80'

def setup_inputs(seed: int=0):
    np.random.seed(seed)
    _w = jnp.asarray

    def _L0_attn_setup():
        import jax, jax.numpy as jnp
        import numpy as np
        N_HEAD = 16
        N_KV_HEAD = 4
        WINDOW = 32
        ROPE_BASE = 10000.0

        def _rotate_half(x):
            h = x.shape[-1] // 2
            return jnp.concatenate([-x[..., h:], x[..., :h]], axis=-1)

        def _rope_cos_sin(T, D):
            inv_freq = 1.0 / ROPE_BASE ** (jnp.arange(0, D, 2, dtype=jnp.float32) / D)
            t = jnp.arange(T, dtype=jnp.float32)
            freqs = t[:, None] * inv_freq[None, :]
            emb = jnp.concatenate([freqs, freqs], axis=-1)
            return (jnp.cos(emb)[None, None], jnp.sin(emb)[None, None])

        def _masks(T, w):
            tq = jnp.arange(T)
            tk = jnp.arange(T)
            causal = tk[None, :] <= tq[:, None]
            i_blk = tq // w * w
            k_start = jnp.maximum(0, i_blk - w // 2)
            upper = tq - (i_blk - k_start)
            local = (tk[None, :] >= k_start[:, None]) & (tk[None, :] <= upper[:, None])
            return (causal, local)
        key = jax.random.key(seed)
        k0, k1, k2, k3, k4 = jax.random.split(key, 5)
        B, T, C = (1, 256, 256)
        D = C // N_HEAD
        s = 0.02
        return {'x': jax.random.normal(k0, (B, T, C), dtype=jnp.float32), 'wq': jax.random.normal(k1, (C, N_HEAD * D), dtype=jnp.float32) * s, 'wk': jax.random.normal(k2, (C, N_KV_HEAD * D), dtype=jnp.float32) * s, 'wv': jax.random.normal(k3, (C, N_KV_HEAD * D), dtype=jnp.float32) * s, 'wo': jax.random.normal(k4, (C, C), dtype=jnp.float32) * s}
    _L0_attn_in = _L0_attn_setup()

    def _L0_ffn_setup():
        import jax, jax.numpy as jnp
        import numpy as np
        K = 2

        def gelu(v):
            return jax.nn.gelu(v, approximate=False)
        key = jax.random.key(seed)
        ks = jax.random.split(key, 10)
        B, S, D, H, E = (4, 256, 256, 128, 8)
        SH = 2 * H
        u = lambda k_, shape, b: jax.random.uniform(k_, shape, jnp.float32, -b, b)
        return {'x': jax.random.normal(ks[0], (B, S, D), jnp.float32), 'gate_w': u(ks[1], (D, E), 1.0 / D), 'w1': u(ks[2], (E, D, H), 1.0 / D), 'b1': u(ks[3], (E, H), 1.0 / np.sqrt(D)), 'w2': u(ks[4], (E, H, D), 1.0 / H), 'b2': u(ks[5], (E, D), 1.0 / np.sqrt(H)), 'shared_w1': u(ks[6], (D, SH), 1.0 / D), 'shared_b1': u(ks[7], (SH,), 1.0 / np.sqrt(D)), 'shared_w2': u(ks[8], (SH, D), 1.0 / SH), 'shared_b2': u(ks[9], (D,), 1.0 / np.sqrt(SH))}
    _L0_ffn_in = _L0_ffn_setup()

    def _L1_attn_setup():
        import jax, jax.numpy as jnp
        import numpy as np
        EPS_L2 = 1e-06
        NORM_EPS = 1e-05

        def short_conv(x, w):
            K = w.shape[1]
            T = x.shape[1]
            xp = jnp.pad(x, ((0, 0), (K - 1, 0), (0, 0)))
            y = xp[:, 0:T, :] * w[:, 0]
            for i in range(1, K):
                y = y + xp[:, i:i + T, :] * w[:, i]
            return jax.nn.silu(y)

        def l2norm(x):
            return x * jax.lax.rsqrt(jnp.sum(x * x, axis=-1, keepdims=True) + EPS_L2)

        def gated_delta_rule(q, k, v, g, beta):

            def per_head(qh, kh, vh, gh, bh):

                def step(S, inp):
                    qt, kt, vt, gt, bt = inp
                    S = S * jnp.exp(gt)
                    delta = (vt - kt @ S) * bt
                    S = S + kt[:, None] * delta[None, :]
                    return (S, qt @ S)
                S0 = jnp.zeros((qh.shape[-1], vh.shape[-1]), jnp.float32)
                _, o = jax.lax.scan(jax.checkpoint(step), S0, (qh, kh, vh, gh, bh))
                return o
            fh = jax.vmap(per_head, in_axes=(1, 1, 1, 1, 1), out_axes=1)
            fb = jax.vmap(fh, in_axes=0, out_axes=0)
            return fb(q, k, v, g, beta)
        key = jax.random.key(seed)
        ks = jax.random.split(key, 16)
        B, T, HID = (1, 128, 256)
        H, DK, DV = (12, 128, 32)
        KDIM, VDIM, KS = (H * DK, H * DV, 4)
        s = 0.02
        hidden_states = jax.random.normal(ks[0], (B, T, HID), jnp.float32)
        Wq = jax.random.normal(ks[1], (HID, KDIM), jnp.float32) * s
        Wk = jax.random.normal(ks[2], (HID, KDIM), jnp.float32) * s
        Wv = jax.random.normal(ks[3], (HID, VDIM), jnp.float32) * s
        Wb = jax.random.normal(ks[4], (HID, H), jnp.float32) * s
        Wa = jax.random.normal(ks[5], (HID, H), jnp.float32) * s
        Wg = jax.random.normal(ks[6], (HID, VDIM), jnp.float32) * s
        Wo = jax.random.normal(ks[7], (VDIM, HID), jnp.float32) * s
        conv_wq = jax.random.normal(ks[8], (KDIM, KS), jnp.float32) * 0.1
        conv_wk = jax.random.normal(ks[9], (KDIM, KS), jnp.float32) * 0.1
        conv_wv = jax.random.normal(ks[10], (VDIM, KS), jnp.float32) * 0.1
        A_log = jnp.log(jax.random.uniform(ks[11], (H,), jnp.float32, 0.5, 8.0))
        dt = jnp.exp(jax.random.uniform(ks[12], (H,), jnp.float32) * (np.log(0.1) - np.log(0.001)) + np.log(0.001))
        dt = jnp.clip(dt, 0.0001, None)
        dt_bias = dt + jnp.log(-jnp.expm1(-dt))
        norm_w = jnp.ones((DV,), jnp.float32)
        return {'hidden_states': hidden_states, 'Wq': Wq, 'Wk': Wk, 'Wv': Wv, 'Wb': Wb, 'Wa': Wa, 'Wg': Wg, 'Wo': Wo, 'conv_wq': conv_wq, 'conv_wk': conv_wk, 'conv_wv': conv_wv, 'A_log': A_log, 'dt_bias': dt_bias, 'norm_w': norm_w}
    _L1_attn_in = _L1_attn_setup()

    def _L1_ffn_setup():
        import jax, jax.numpy as jnp
        import numpy as np
        B, S, H = (1, 256, 256)
        E, K, I = (16, 4, 176)
        IS = 352
        CAP = 128
        key = jax.random.key(seed)
        ks = jax.random.split(key, 8)
        sc = 0.02
        return {'hidden_states': jax.random.normal(ks[0], (B, S, H), jnp.float32), 'gate_w': jax.random.normal(ks[1], (E, H), jnp.float32) * sc, 'w_gate': jax.random.normal(ks[2], (E, H, I), jnp.float32) * sc, 'w_up': jax.random.normal(ks[3], (E, H, I), jnp.float32) * sc, 'w_down': jax.random.normal(ks[4], (E, I, H), jnp.float32) * sc, 'sw_gate': jax.random.normal(ks[5], (H, IS), jnp.float32) * sc, 'sw_up': jax.random.normal(ks[6], (H, IS), jnp.float32) * sc, 'sw_down': jax.random.normal(ks[7], (IS, H), jnp.float32) * sc}
    _L1_ffn_in = _L1_ffn_setup()
    _d = {'L0_attn_x': _L0_attn_in['x'], 'L0_attn_wq': _L0_attn_in['wq'], 'L0_attn_wk': _L0_attn_in['wk'], 'L0_attn_wv': _L0_attn_in['wv'], 'L0_attn_wo': _L0_attn_in['wo'], 'L0_ffn_gate_w': _L0_ffn_in['gate_w'], 'L0_ffn_w1': _L0_ffn_in['w1'], 'L0_ffn_b1': _L0_ffn_in['b1'], 'L0_ffn_w2': _L0_ffn_in['w2'], 'L0_ffn_b2': _L0_ffn_in['b2'], 'L0_ffn_shared_w1': _L0_ffn_in['shared_w1'], 'L0_ffn_shared_b1': _L0_ffn_in['shared_b1'], 'L0_ffn_shared_w2': _L0_ffn_in['shared_w2'], 'L0_ffn_shared_b2': _L0_ffn_in['shared_b2'], 'L1_attn_Wq': _L1_attn_in['Wq'], 'L1_attn_Wk': _L1_attn_in['Wk'], 'L1_attn_Wv': _L1_attn_in['Wv'], 'L1_attn_Wb': _L1_attn_in['Wb'], 'L1_attn_Wa': _L1_attn_in['Wa'], 'L1_attn_Wg': _L1_attn_in['Wg'], 'L1_attn_Wo': _L1_attn_in['Wo'], 'L1_attn_conv_wq': _L1_attn_in['conv_wq'], 'L1_attn_conv_wk': _L1_attn_in['conv_wk'], 'L1_attn_conv_wv': _L1_attn_in['conv_wv'], 'L1_attn_A_log': _L1_attn_in['A_log'], 'L1_attn_dt_bias': _L1_attn_in['dt_bias'], 'L1_attn_norm_w': _L1_attn_in['norm_w'], 'L1_ffn_gate_w': _L1_ffn_in['gate_w'], 'L1_ffn_w_gate': _L1_ffn_in['w_gate'], 'L1_ffn_w_up': _L1_ffn_in['w_up'], 'L1_ffn_w_down': _L1_ffn_in['w_down'], 'L1_ffn_sw_gate': _L1_ffn_in['sw_gate'], 'L1_ffn_sw_up': _L1_ffn_in['sw_up'], 'L1_ffn_sw_down': _L1_ffn_in['sw_down']}
    _x0 = _d['L0_attn_x']
    _d['L0_attn_x'] = jax.random.normal(jax.random.fold_in(jax.random.key(seed), 1), (4, 512, 256), dtype=_x0.dtype)
    del _x0
    return _d

def reference(L0_attn_x, L0_attn_wq, L0_attn_wk, L0_attn_wv, L0_attn_wo, L0_ffn_gate_w, L0_ffn_w1, L0_ffn_b1, L0_ffn_w2, L0_ffn_b2, L0_ffn_shared_w1, L0_ffn_shared_b1, L0_ffn_shared_w2, L0_ffn_shared_b2, L1_attn_Wq, L1_attn_Wk, L1_attn_Wv, L1_attn_Wb, L1_attn_Wa, L1_attn_Wg, L1_attn_Wo, L1_attn_conv_wq, L1_attn_conv_wk, L1_attn_conv_wv, L1_attn_A_log, L1_attn_dt_bias, L1_attn_norm_w, L1_ffn_gate_w, L1_ffn_w_gate, L1_ffn_w_up, L1_ffn_w_down, L1_ffn_sw_gate, L1_ffn_sw_up, L1_ffn_sw_down):

    def _L0_attn_ref(x, wq, wk, wv, wo):
        import jax, jax.numpy as jnp
        import numpy as np
        N_HEAD = 16
        N_KV_HEAD = 4
        WINDOW = 32
        ROPE_BASE = 10000.0

        def _rotate_half(x):
            h = x.shape[-1] // 2
            return jnp.concatenate([-x[..., h:], x[..., :h]], axis=-1)

        def _rope_cos_sin(T, D):
            inv_freq = 1.0 / ROPE_BASE ** (jnp.arange(0, D, 2, dtype=jnp.float32) / D)
            t = jnp.arange(T, dtype=jnp.float32)
            freqs = t[:, None] * inv_freq[None, :]
            emb = jnp.concatenate([freqs, freqs], axis=-1)
            return (jnp.cos(emb)[None, None], jnp.sin(emb)[None, None])

        def _masks(T, w):
            tq = jnp.arange(T)
            tk = jnp.arange(T)
            causal = tk[None, :] <= tq[:, None]
            i_blk = tq // w * w
            k_start = jnp.maximum(0, i_blk - w // 2)
            upper = tq - (i_blk - k_start)
            local = (tk[None, :] >= k_start[:, None]) & (tk[None, :] <= upper[:, None])
            return (causal, local)
        B, T, C = x.shape
        D = C // N_HEAD
        g = N_HEAD // N_KV_HEAD
        q = (x @ wq).reshape(B, T, N_HEAD, D)
        k = (x @ wk).reshape(B, T, N_KV_HEAD, D)
        v = (x @ wv).reshape(B, T, N_KV_HEAD, D)
        k = jnp.repeat(k, g, axis=2)
        v = jnp.repeat(v, g, axis=2)
        q = q.transpose(0, 2, 1, 3)
        k = k.transpose(0, 2, 1, 3)
        v = v.transpose(0, 2, 1, 3)
        cos, sin = _rope_cos_sin(T, D)
        q = q * cos + _rotate_half(q) * sin
        k = k * cos + _rotate_half(k) * sin
        scale = 1.0 / jnp.sqrt(jnp.asarray(D, dtype=q.dtype))
        scores = jnp.einsum('bhqd,bhkd->bhqk', q, k) * scale
        causal, local = _masks(T, WINDOW)
        neg = jnp.finfo(scores.dtype).min
        p_g = jax.nn.softmax(jnp.where(causal, scores, neg), axis=-1)
        p_l = jax.nn.softmax(jnp.where(local, scores, neg), axis=-1)
        out_g = jnp.einsum('bhqk,bhkd->bhqd', p_g, v)
        out_l = jnp.einsum('bhqk,bhkd->bhqd', p_l, v)
        out = 0.5 * (out_g + out_l)
        out = out.transpose(0, 2, 1, 3).reshape(B, T, C)
        return out @ wo

    def _L0_ffn_ref(x, gate_w, w1, b1, w2, b2, shared_w1, shared_b1, shared_w2, shared_b2):
        import jax, jax.numpy as jnp
        import numpy as np
        K = 2

        def gelu(v):
            return jax.nn.gelu(v, approximate=False)
        B, S, D = x.shape
        E = gate_w.shape[1]
        xf = x.reshape(-1, D)
        logits = xf @ gate_w
        top_logits, top_idx = jax.lax.top_k(logits, K)
        top_gates = jax.nn.softmax(top_logits, axis=-1)
        gates = jnp.sum(jax.nn.one_hot(top_idx, E, dtype=xf.dtype) * top_gates[..., None], axis=1)
        h = gelu(jnp.einsum('nd,edh->neh', xf, w1) + b1)
        out_e = jnp.einsum('neh,ehd->ned', h, w2) + b2
        routed = jnp.einsum('ne,ned->nd', gates, out_e)
        shared = gelu(xf @ shared_w1 + shared_b1) @ shared_w2 + shared_b2
        return (routed + shared).reshape(B, S, D)

    def _L1_attn_ref(hidden_states, Wq, Wk, Wv, Wb, Wa, Wg, Wo, conv_wq, conv_wk, conv_wv, A_log, dt_bias, norm_w):
        import jax, jax.numpy as jnp
        import numpy as np
        EPS_L2 = 1e-06
        NORM_EPS = 1e-05

        def short_conv(x, w):
            K = w.shape[1]
            T = x.shape[1]
            xp = jnp.pad(x, ((0, 0), (K - 1, 0), (0, 0)))
            y = xp[:, 0:T, :] * w[:, 0]
            for i in range(1, K):
                y = y + xp[:, i:i + T, :] * w[:, i]
            return jax.nn.silu(y)

        def l2norm(x):
            return x * jax.lax.rsqrt(jnp.sum(x * x, axis=-1, keepdims=True) + EPS_L2)

        def gated_delta_rule(q, k, v, g, beta):

            def per_head(qh, kh, vh, gh, bh):

                def step(S, inp):
                    qt, kt, vt, gt, bt = inp
                    S = S * jnp.exp(gt)
                    delta = (vt - kt @ S) * bt
                    S = S + kt[:, None] * delta[None, :]
                    return (S, qt @ S)
                S0 = jnp.zeros((qh.shape[-1], vh.shape[-1]), jnp.float32)
                _, o = jax.lax.scan(jax.checkpoint(step), S0, (qh, kh, vh, gh, bh))
                return o
            fh = jax.vmap(per_head, in_axes=(1, 1, 1, 1, 1), out_axes=1)
            fb = jax.vmap(fh, in_axes=0, out_axes=0)
            return fb(q, k, v, g, beta)
        B, T, _ = hidden_states.shape
        H = A_log.shape[0]
        q = short_conv(hidden_states @ Wq, conv_wq)
        k = short_conv(hidden_states @ Wk, conv_wk)
        v = short_conv(hidden_states @ Wv, conv_wv)
        q = l2norm(q.reshape(B, T, H, -1))
        k = l2norm(k.reshape(B, T, H, -1))
        v = v.reshape(B, T, H, -1)
        beta = jax.nn.sigmoid(hidden_states @ Wb)
        g = -jnp.exp(A_log) * jax.nn.softplus(hidden_states @ Wa + dt_bias)
        o = gated_delta_rule(q, k, v, g, beta)
        gg = (hidden_states @ Wg).reshape(B, T, H, -1)
        o_n = o * jax.lax.rsqrt(jnp.mean(o * o, axis=-1, keepdims=True) + NORM_EPS) * norm_w
        o_n = o_n * jax.nn.silu(gg)
        return o_n.reshape(B, T, -1) @ Wo

    def _L1_ffn_ref(hidden_states, gate_w, w_gate, w_up, w_down, sw_gate, sw_up, sw_down):
        import jax, jax.numpy as jnp
        import numpy as np
        B, S, H = (1, 256, 256)
        E, K, I = (16, 4, 176)
        IS = 352
        CAP = 128
        b, s, h = hidden_states.shape
        x = hidden_states.reshape(-1, h)
        T = x.shape[0]
        scores = jax.nn.softmax(x @ gate_w.T, axis=-1)
        topk_w, topk_i = jax.lax.top_k(scores, K)
        topk_w = topk_w / (topk_w.sum(-1, keepdims=True) + 1e-20)
        flat_i = topk_i.reshape(-1)
        flat_w = topk_w.reshape(-1)
        order = jnp.argsort(flat_i)
        se = flat_i[order]
        counts = jax.ops.segment_sum(jnp.ones_like(flat_i), flat_i, num_segments=E)
        starts = jnp.cumsum(counts) - counts
        rank = jnp.arange(T * K) - starts[se]
        tok = order // K
        slot = jnp.where(rank < CAP, rank, CAP)
        buf = jnp.full((E, CAP + 1), T, dtype=jnp.int32).at[se, slot].set(tok)[:, :CAP]
        wbuf = jnp.zeros((E, CAP + 1), x.dtype).at[se, slot].set(flat_w[order])[:, :CAP]
        xpad = jnp.concatenate([x, jnp.zeros((1, h), x.dtype)], axis=0)
        xg = xpad[buf]
        gact = jax.nn.silu(jnp.einsum('ech,ehi->eci', xg, w_gate))
        mid = gact * jnp.einsum('ech,ehi->eci', xg, w_up)
        eout = jnp.einsum('eci,eih->ech', mid, w_down) * wbuf[..., None]
        y = jnp.zeros((T + 1, h), x.dtype).at[buf.reshape(-1)].add(eout.reshape(-1, h))[:T]
        shared = jax.nn.silu(x @ sw_gate) * (x @ sw_up) @ sw_down
        return (y + shared).reshape(b, s, h)
    x = L0_attn_x
    x = _layernorm(x + _L0_attn_ref(x, L0_attn_wq, L0_attn_wk, L0_attn_wv, L0_attn_wo), axis=-1)
    x = _layernorm(x + _L0_ffn_ref(x, L0_ffn_gate_w, L0_ffn_w1, L0_ffn_b1, L0_ffn_w2, L0_ffn_b2, L0_ffn_shared_w1, L0_ffn_shared_b1, L0_ffn_shared_w2, L0_ffn_shared_b2), axis=-1)
    x = _layernorm(x + _L1_attn_ref(x, L1_attn_Wq, L1_attn_Wk, L1_attn_Wv, L1_attn_Wb, L1_attn_Wa, L1_attn_Wg, L1_attn_Wo, L1_attn_conv_wq, L1_attn_conv_wk, L1_attn_conv_wv, L1_attn_A_log, L1_attn_dt_bias, L1_attn_norm_w), axis=-1)
    x = _layernorm(x + _L1_ffn_ref(x, L1_ffn_gate_w, L1_ffn_w_gate, L1_ffn_w_up, L1_ffn_w_down, L1_ffn_sw_gate, L1_ffn_sw_up, L1_ffn_sw_down), axis=-1)
    return x

_drawn_inputs = setup_inputs


def setup_inputs(seed=0):
    import zlib

    import numpy as np

    out = dict(_drawn_inputs(seed))
    spreads = {'L1_attn_norm_w': (1.0, 0.6)}
    factors = {'L0_attn_wq': 8.0,
     'L0_attn_wk': 8.0,
     'L0_ffn_w1': 8.0,
     'L0_ffn_b1': 8.0,
     'L0_ffn_w2': 8.0,
     'L0_ffn_shared_w1': 8.0,
     'L0_ffn_shared_b1': 8.0,
     'L0_ffn_shared_w2': 8.0,
     'L1_attn_Wb': 7.14,
     'L1_attn_Wa': 8.0,
     'L1_attn_A_log': 5.455,
     'L1_ffn_gate_w': 8.0,
     'L1_ffn_w_gate': 8.0,
     'L1_ffn_w_up': 8.0,
     'L1_ffn_w_down': 8.0,
     'L1_ffn_sw_gate': 2.893,
     'L1_ffn_sw_up': 2.862,
     'L1_ffn_sw_down': 2.856}
    for name, (base, spread) in spreads.items():
        noise = np.random.default_rng([zlib.crc32(name.encode()), seed]).standard_normal(out[name].shape)
        drawn = base * np.exp(spread * noise) if base else spread * noise
        out[name] = jnp.asarray(drawn.astype(out[name].dtype))
    for name, factor in factors.items():
        out[name] = (out[name] * factor).astype(out[name].dtype)
    return out
```

```python
import numpy as np
from contextlib import ExitStack
import concourse.bass as bass
from concourse import mybir

F32 = mybir.dt.float32
BF16 = mybir.dt.bfloat16
ALU = mybir.AluOpType
ACT = mybir.ActivationFunctionType
AX = mybir.AxisListType

P = 128
BATCH, T, C = 4, 512, 256
NT = T // P
TILES = BATCH * NT
CK = C // P
EPS_LN = 1e-5
A_HEADS, A_KV, A_D, WINDOW = 16, 4, 16, 32
A_ROT = A_HEADS + A_KV
A_QKV = (A_HEADS + 2 * A_KV) * A_D
A_SCALE = A_D ** -0.5
Q_PARTS = [0, 0, 0, 1, 1, 1, 2, 2]
K_PARTS = [0, 1, 2, 0, 1, 2, 0, 1]
HALF = WINDOW // 2
NEG = -1.0e30
K_CHAIN = 7 * NT + 5 + 2 * A_KV + 2


def in_bf16(a):
    return a.astype(mybir.dt.np(BF16))


def constants():
    out = {}
    i = np.arange(P)
    out["c_ident"] = np.eye(P, dtype=np.float32)
    out["c_identb"] = in_bf16(np.eye(P))
    inv = (np.float32(1.0) / np.float32(10000.0) ** (np.arange(0, A_D, 2, dtype=np.float32) / np.float32(A_D))).astype(np.float32)
    ang = np.arange(T, dtype=np.float32)[:, None] * inv[None, :]
    cs = np.stack([np.cos(ang), -np.sin(ang), np.sin(ang)], 1).astype(np.float32)
    out["c_rope"] = np.ascontiguousarray(cs.reshape(NT, P, 3, A_D // 2).transpose(1, 0, 2, 3))
    causal = np.where(i[None, :] <= i[:, None], 0.0, NEG)
    q, w = i[:, None], i[None, :]
    later = (w >= q // WINDOW * WINDOW) & (w <= q)
    first = np.where(q < WINDOW, w <= q, (w >= q // WINDOW * WINDOW - HALF) & (w <= q - HALF))
    later, first = (np.where(m, 0.0, NEG) for m in (later, first))
    out["c_qmask"] = in_bf16(np.stack([causal, first, later, later, later], 1))
    out["c_kmask"] = in_bf16(np.stack([causal.T, first.T, later.T, later.T, later.T], 1))
    sel = np.zeros((A_HEADS, 3, A_HEADS, P))
    for h in range(A_HEADS):
        sel[h, :, h, :] = 1.0
    out["c_sel"] = in_bf16(sel.reshape(3 * A_HEADS, A_HEADS, P))
    return out


def window_start(i):
    return P * i - HALF if i else 0


def layer0_attention(nc, d):
    ctx, sems = ExitStack(), []
    with ctx:
        def sb(name, shape, dt=F32):
            return ctx.enter_context(nc.sbuf_tensor("a_" + name, shape, dt))

        def pb(name, shape, dt=F32):
            return ctx.enter_context(nc.psum_tensor("a_" + name, shape, dt))

        def sem(name):
            sems.append(nc.alloc_semaphore("a_" + name))
            return sems[-1]

        ident, identb = sb("ident", [P, P]), sb("identb", [P, P], BF16)
        rope = sb("rope", [P, NT, 3, A_D // 2])
        qmask, kmask = sb("qmask", [P, 5, P], BF16), sb("kmask", [P, 5, P], BF16)
        sel = sb("sel", [3 * A_HEADS, A_HEADS, P], BF16)
        w_qkv, w_o = sb("w_qkv", [P, CK, A_QKV]), sb("w_o", [P, CK, C])
        x, xT = sb("x", [P, NT, C]), sb("xT", [P, CK, T])
        t_cos, t_sin = sb("t_cos", [P, A_ROT, A_D]), sb("t_sin", [P, A_ROT, A_D])
        rot, rest = sb("rot", [P, A_ROT, A_D]), sb("rest", [P, A_ROT, A_D])
        parts = sb("parts", [P, 2, 3, A_ROT, A_D], BF16)
        stack = sb("stack", [P, NT, A_ROT, 8, A_D], BF16)
        qS, kS = sb("qS", [P, A_HEADS, T], BF16), sb("kS", [P, A_KV, T], BF16)
        v_tile, v_win = sb("v_tile", [P, NT, A_KV, 32]), sb("v_win", [P, NT, A_KV, 32])
        top = sb("top", [P, 2, NT, A_HEADS])
        ntop, nrest = sb("ntop", [P, 2, NT, A_HEADS]), sb("nrest", [P, 2, NT, A_HEADS])
        nparts = sb("nparts", [P, 2, NT, A_HEADS, 3], BF16)
        ntopT = sb("ntopT", [3 * A_HEADS, 2, T], BF16)
        probs = sb("probs", [P, 2, 2, 1024])
        ot = sb("ot", [P, 2, T])
        inv_z, scaled = sb("inv_z", [P, 2, NT, 4]), sb("scaled", [P, 2, NT, 4, A_D])
        mixed, mixedT = sb("mixed", [P, NT, A_HEADS * A_D]), sb("mixedT", [P, CK, T])
        y, x1 = sb("y", [P, NT, C]), sb("x1", [P, NT, C])
        stats, mean_var = sb("stats", [P, NT, 6]), sb("mean_var", [P, NT, 2])
        rstd, mhalf = sb("rstd", [P, NT]), sb("mhalf", [P, NT])

        TB = [pb(f"turn{n}", [P, T]) for n in range(2)]
        AB = [pb(f"acc{n}", [P, 2, T]) for n in range(2)]
        CB = [pb(f"out{n}", [P, T]) for n in range(2)]
        TBh = [t[:].bitcast(BF16) for t in TB]

        loaded, x_in, x_turned, xT_ready = sem("loaded"), sem("x_in"), sem("x_turned"), sem("xT_ready")
        projected, split, chain, v_copied = sem("projected"), sem("split"), sem("chain"), sem("v_copied")
        dup_act, dup_pool, stacked = sem("dup_act"), sem("dup_pool"), sem("stacked")
        ev_act, ev_dve = sem("ev_act"), sem("ev_dve")
        scored, maxed, nsplit, nturned, nT_ready = sem("scored"), sem("maxed"), sem("nsplit"), sem("nturned"), sem("nT_ready")
        ot_ready, ot_turned = sem("ot_ready"), sem("ot_turned")
        rescored, expd, pv_done, normed = sem("rescored"), sem("expd"), sem("pv_done"), sem("normed")
        o_turned, oT_ready, o_proj, resid = sem("o_turned"), sem("oT_ready"), sem("o_proj"), sem("resid")
        var_ready, rstd_ready, ln_done, stored, ones = sem("var_ready"), sem("rstd_ready"), sem("ln_done"), sem("stored"), sem("ones")
        U1 = NT * A_HEADS // 2
        U = U1 + A_HEADS // 2
        NST = A_ROT // 2
        x_b = d["L0_attn_x"].rearrange("b (t p) c -> b p t c", p=P)
        x1_b = d["x1"].rearrange("(b t p) c -> b p t c", p=P, t=NT)

        carrier_pe, carrier_pool, carrier_dve = (sem("carrier_" + n) for n in ("pe", "pool", "dve"))
        block = ctx.enter_context(nc.Block())

        @block.sync
        def _(sp):
            for dst, src in ((ident[:], d["c_ident"]), (identb[:], d["c_identb"]), (rope[:], d["c_rope"]),
                             (qmask[:], d["c_qmask"]), (kmask[:], d["c_kmask"]), (sel[:], d["c_sel"]),
                             (w_qkv[:, :, 0:C], d["L0_attn_wq"].rearrange("(k p) n -> p k n", p=P)),
                             (w_qkv[:, :, C:C + 64], d["L0_attn_wk"].rearrange("(k p) n -> p k n", p=P)),
                             (w_qkv[:, :, C + 64:C + 128], d["L0_attn_wv"].rearrange("(k p) n -> p k n", p=P)),
                             (w_o[:], d["L0_attn_wo"].rearrange("(k p) n -> p k n", p=P))):
                sp.dma_start(dst, src).then_inc(loaded, 16)
            with sp.Fori(0, BATCH) as b:
                sp.wait_ge(resid, b)
                sp.dma_start(x[:], x_b[b, :, :, :]).then_inc(x_in, 16)

        @block.tensor
        def _(pe):
            pe.wait_ge(loaded, 160)
            with pe.Fori(0, BATCH) as b:
                pe.wait_ge(x_in, 16 * b + 16)
                pe.wait_ge(oT_ready, 2 * b)
                for k in range(CK):
                    for t in range(NT):
                        last = nc.tensor.transpose(TB[k][:, t * P:(t + 1) * P], x[:, t, k * P:(k + 1) * P], ident[:])
                last.then_inc(x_turned, 1)
                pe.wait_ge(xT_ready, 2 * b + 2)
                pe.wait_ge(resid, b)
                for t in range(NT):
                    for k in range(CK):
                        last = nc.tensor.matmul(AB[t // 2][:, t % 2, 0:A_QKV], xT[:, k, t * P:(t + 1) * P],
                                                w_qkv[:, k, :], start=k == 0, stop=k == CK - 1)
                    last.then_inc(projected, 1)
                for t in range(NT):
                    s = window_start(t)
                    for k in range(CK):
                        last = nc.tensor.matmul(CB[0][:, t * 64:t * 64 + 64],
                                                xT[:, k, s:s + P], w_qkv[:, k, A_QKV - 64:A_QKV],
                                                start=k == 0, stop=k == CK - 1)
                last.then_inc(projected, 1)
                pe.wait_ge(dup_act, NT * b + NT)
                pe.wait_ge(dup_pool, NT * b + NT)
                for n in range(NST):
                    if n >= 2:
                        pe.wait_ge(ev_act if n % 2 == 0 else ev_dve, NST // 2 * b + n // 2)
                    for a in range(2):
                        head = (A_HEADS + 2 * n if n < 2 else 2 * (n - 2)) + a
                        for t in range(NT):
                            last = nc.tensor.transpose(TBh[n % 2][:, a * T + t * P:a * T + (t + 1) * P],
                                                       stack[:, t, head, :, :].rearrange("p s d -> p (s d)"), identb[:])
                    last.then_inc(stacked, 1)
                pe.wait_ge(ev_act, NST // 2 * (b + 1))
                pe.wait_ge(ev_dve, NST // 2 * (b + 1))
                for u in range(U):
                    if u >= 2:
                        pe.wait_ge(maxed, U * b + u - 1)
                    for a in range(2):
                        acc = AB[u % 2][:, a, :]
                        if u < U1:
                            i, h = u // 8, 2 * (u % 8) + a
                            w = P * (i + 1)
                            nc.tensor.matmul(acc[:, 0:w], qS[:, h, i * P:(i + 1) * P], kS[:, h // 4, 0:w], start=True, stop=False)
                            last = nc.tensor.matmul(acc[:, w - P:w], identb[:], qmask[:, 0, :], start=False, stop=True)
                        else:
                            h = 2 * (u - U1) + a
                            for i in range(NT):
                                s = window_start(i)
                                nc.tensor.matmul(acc[:, i * P:(i + 1) * P], qS[:, h, i * P:(i + 1) * P],
                                                 kS[:, h // 4, s:s + P], start=True, stop=False)
                                last = nc.tensor.matmul(acc[:, i * P:(i + 1) * P], identb[:], qmask[:, 1 + i, :],
                                                        start=False, stop=True)
                    last.then_inc(scored, 1)
                pe.wait_ge(nsplit, b + 1)
                pe.sem_inc(carrier_pe)
                for g in range(2):
                    for t in range(NT):
                        last = nc.tensor.transpose(TBh[0][0:3 * A_HEADS, g * T + t * P:g * T + (t + 1) * P],
                                                   nparts[:, g, t, :, :].rearrange("p h s -> p (h s)"), identb[:])
                last.then_inc(nturned, 1)
                pe.wait_ge(nT_ready, b + 1)
                pe.wait_ge(maxed, U * (b + 1))

                def weigh(h):
                    pe.wait_ge(expd, 2 * A_HEADS * b + 2 * h + 2)
                    if h % 4 == 0 and h:
                        pe.wait_ge(ot_ready, 2 * A_KV * b + h // 2)
                    p0, p1 = probs[:, h % 2, 0, :], probs[:, h % 2, 1, :]
                    past = [p1[:, 0:T], p1[:, T:T + 384], p0[:, T:T + 256], p0[:, T + 256:T + 384]]
                    rows = slice(32 * (h % 4), 32 * (h % 4) + 32)
                    for j in range(NT):
                        nc.tensor.matmul(CB[0][rows, j * P:T], v_tile[:, j, h // 4, :], past[j], start=j == 0, stop=j == NT - 1)
                    for i in range(NT):
                        last = nc.tensor.matmul(CB[1][rows, i * P:(i + 1) * P], v_win[:, i, h // 4, :], p0[:, i * P:(i + 1) * P],
                                                start=True, stop=True)
                    last.then_inc(pv_done, 1)

                def turn_back(g):
                    pe.wait_ge(ot_ready, 2 * A_KV * b + 2 * g + 2)
                    if g:
                        pe.wait_ge(normed, A_KV * b + g)
                    for a in range(2):
                        for t in range(NT):
                            last = nc.tensor.transpose(TB[a][:, t * P:(t + 1) * P], ot[:, a, t * P:(t + 1) * P], ident[:])
                    last.then_inc(ot_turned, 1)

                for h in range(A_HEADS):
                    g = h // 4
                    for u in range(2):
                        if h >= 1:
                            pe.wait_ge(expd, 2 * A_HEADS * b + 2 * h + u - 1)
                        a0, a1 = AB[u][:, 0, :], AB[u][:, 1, :]
                        if u == 0:
                            nc.tensor.matmul(a0, sel[:, h, :], ntopT[:, 1, :], start=True, stop=False)
                            for i in range(NT):
                                s = window_start(i)
                                nc.tensor.matmul(a0[:, i * P:(i + 1) * P], kS[:, g, s:s + P], qS[:, h, i * P:(i + 1) * P],
                                                 start=False, stop=False)
                            nc.tensor.matmul(a0, identb[:], kmask[:, 1:5, :].rearrange("p a q -> p (a q)"), start=False, stop=True)
                            nc.tensor.matmul(a1[:, 0:256], sel[:, h, :], ntopT[:, 0, 256:512], start=True, stop=False)
                            nc.tensor.matmul(a1[:, 256:384], sel[:, h, :], ntopT[:, 0, 384:512], start=False, stop=False)
                            nc.tensor.matmul(a1[:, 0:256], kS[:, g, 256:384], qS[:, h, 256:512], start=False, stop=False)
                            nc.tensor.matmul(a1[:, 256:384], kS[:, g, 384:512], qS[:, h, 384:512], start=False, stop=False)
                            nc.tensor.matmul(a1[:, 0:128], identb[:], kmask[:, 0, :], start=False, stop=False)
                            last = nc.tensor.matmul(a1[:, 256:384], identb[:], kmask[:, 0, :], start=False, stop=True)
                        else:
                            for j, a in ((0, a0), (1, a1)):
                                w = T - P * j
                                nc.tensor.matmul(a[:, 0:w], sel[:, h, :], ntopT[:, 0, P * j:T], start=True, stop=False)
                                nc.tensor.matmul(a[:, 0:w], kS[:, g, P * j:P * (j + 1)], qS[:, h, P * j:T], start=False, stop=False)
                                last = nc.tensor.matmul(a[:, 0:P], identb[:], kmask[:, 0, :], start=False, stop=True)
                        last.then_inc(rescored, 1)
                    if h >= 1:
                        weigh(h - 1)
                    if h % 4 == 1 and h > 4:
                        turn_back(h // 4 - 1)
                weigh(A_HEADS - 1)
                turn_back(A_KV - 1)
                pe.wait_ge(normed, A_KV * (b + 1))
                for k in range(CK):
                    for t in range(NT):
                        last = nc.tensor.transpose(TB[k][:, t * P:(t + 1) * P], mixed[:, t, k * P:(k + 1) * P], ident[:])
                last.then_inc(o_turned, 1)
                pe.wait_ge(oT_ready, 2 * b + 2)
                for t in range(NT):
                    for k in range(CK):
                        last = nc.tensor.matmul(AB[0][:, t // 2, t % 2 * C:t % 2 * C + C], mixedT[:, k, t * P:(t + 1) * P],
                                                w_o[:, k, :], start=k == 0, stop=k == CK - 1)
                last.then_inc(o_proj, 1)

        @block.scalar
        def _(act):
            act.wait_ge(loaded, 160)
            act.wait_ge(ones, 3)
            with act.Fori(0, BATCH) as b:
                act.wait_ge(x_turned, b + 1)
                for k in range(CK):
                    nc.scalar.activation(xT[:, k, :], TB[k][:], ACT.Copy).then_inc(xT_ready, 1)
                for t in range(NT):
                    act.wait_ge(split, NT * b + t + 1)
                    nc.scalar.activation(v_tile[:, t, :, 0:A_D], AB[t // 2][:, t % 2, A_QKV - 64:A_QKV]
                                         .rearrange("p (g d) -> p g d", g=A_KV), ACT.Copy).then_inc(v_copied, 1)
                    pt = parts[:, t % 2, :, :, :]
                    last = None
                    for lo, hi, part in ((0, 3, 0), (3, 6, 1)):
                        for s in range(lo, hi):
                            last = nc.scalar.activation(stack[:, t, 0:A_HEADS, s, :], pt[:, part, 0:A_HEADS, :], ACT.Copy)
                    last.then_inc(dup_act, 1)
                act.wait_ge(projected, 5 * b + 5)
                nc.scalar.activation(v_win[:, :, :, 0:A_D], CB[0][:, 0:256]
                                     .rearrange("p (t g d) -> p t g d", t=NT, g=A_KV), ACT.Copy).then_inc(v_copied, 1)
                for n in range(0, NST, 2):
                    act.wait_ge(stacked, NST * b + n + 1)
                    dst = kS[:, 0:2, :] if n == 0 else qS[:, 2 * (n - 2):2 * (n - 2) + 2, :]
                    nc.scalar.activation(dst, TBh[0].rearrange("p (a t) -> p a t", a=2), ACT.Copy).then_inc(ev_act, 1)
                act.wait_ge(nturned, b + 1)
                nc.scalar.activation(ntopT[:], TBh[0][0:3 * A_HEADS, :].rearrange("p (a t) -> p a t", a=2), ACT.Copy)\
                    .then_inc(nT_ready, 1)
                for h in range(A_HEADS):
                    for u in range(2):
                        act.wait_ge(rescored, 2 * A_HEADS * b + 2 * h + u + 1)
                        if h >= 2 and u == 0:
                            act.wait_ge(pv_done, A_HEADS * b + h - 1)
                        nc.scalar.activation(probs[:, h % 2, u, 0:896], AB[u][:].rearrange("p a t -> p (a t)")[:, 0:896],
                                             ACT.Exp, scale=A_SCALE).then_inc(expd, 1)
                act.wait_ge(o_turned, b + 1)
                for k in range(CK):
                    nc.scalar.activation(mixedT[:, k, :], TB[k][:], ACT.Copy).then_inc(oT_ready, 1)

        @block.gpsimd
        def _(pool):
            nc.gpsimd.memset(v_tile[:], 2.0).then_inc(ones, 1)
            nc.gpsimd.memset(v_win[:], 2.0).then_inc(ones, 1)
            nc.gpsimd.memset(mhalf[:], -0.5).then_inc(ones, 1)
            pool.wait_ge(ones, 3)
            with pool.Fori(0, BATCH) as b:
                for t in range(NT):
                    pool.wait_ge(split, NT * b + t + 1)
                    pool.sem_inc(carrier_pool)
                    pt = parts[:, t % 2, :, :, :]
                    for s in range(8):
                        last = nc.gpsimd.tensor_scalar(stack[:, t, A_HEADS:A_ROT, s, :], pt[:, K_PARTS[s], A_HEADS:A_ROT, :],
                                                       1.0, 0.0, ALU.mult, ALU.add)
                    for s in (6, 7):
                        last = nc.gpsimd.tensor_scalar(stack[:, t, 0:A_HEADS, s, :], pt[:, 2, 0:A_HEADS, :],
                                                       1.0, 0.0, ALU.mult, ALU.add)
                    last.then_inc(dup_pool, 1)
                pool.wait_ge(var_ready, b + 1)
                nc.gpsimd.tensor_tensor(rstd[:], rstd[:], mhalf[:], ALU.pow).then_inc(rstd_ready, 1)
                pool.wait_ge(ln_done, b + 1)
                pool.sem_inc(carrier_pool)
                pool.dma_start(x1_b[b, :, :, :], x1[:]).then_inc(stored, 16)
            pool.wait_ge(stored, 16 * BATCH)

        @block.vector
        def _(dve):
            dve.wait_ge(loaded, 160)
            with dve.Fori(0, BATCH) as b:
                count = [0]

                def link(ins):
                    count[0] += 1
                    ins.then_inc(chain, 1)
                    dve.wait_ge(chain, K_CHAIN * b + count[0])

                for t in range(NT):
                    dve.wait_ge(projected, 5 * b + t + 1)
                    src = AB[t // 2][:, t % 2, 0:A_ROT * A_D].rearrange("p (h e d) -> p h e d", h=A_ROT, e=2)
                    cos = rope[:, t, 0:1, None, :].broadcast_to([P, A_ROT, 2, A_D // 2])
                    link(nc.vector.tensor_tensor(t_cos[:].rearrange("p h (e d) -> p h e d", e=2), src, cos, ALU.mult))
                    for e in range(2):
                        sin = rope[:, t, 1 + e:2 + e, :].broadcast_to([P, A_ROT, A_D // 2])
                        ins = nc.vector.tensor_tensor(t_sin[:, :, 8 * e:8 * e + 8], src[:, :, 1 - e, :], sin, ALU.mult)
                    link(ins)
                    link(nc.vector.tensor_tensor(rot[:], t_cos[:], t_sin[:], ALU.add))
                    pt = parts[:, t % 2, :, :, :]
                    if t >= 2:
                        dve.wait_ge(dup_act, NT * b + t - 1)
                        dve.wait_ge(dup_pool, NT * b + t - 1)
                    link(nc.vector.tensor_copy(pt[:, 0, :, :], rot[:]))
                    link(nc.vector.tensor_tensor(rest[:], rot[:], pt[:, 0, :, :], ALU.subtract))
                    link(nc.vector.tensor_copy(pt[:, 1, :, :], rest[:]))
                    link(nc.vector.tensor_tensor(rest[:], rest[:], pt[:, 1, :, :], ALU.subtract))
                    nc.vector.tensor_copy(pt[:, 2, :, :], rest[:]).then_inc(split, 1)
                for n in range(1, NST, 2):
                    dve.wait_ge(stacked, NST * b + n + 1)
                    dst = kS[:, 2:4, :] if n == 1 else qS[:, 2 * (n - 2):2 * (n - 2) + 2, :]
                    nc.vector.tensor_copy(dst, TBh[1].rearrange("p (a t) -> p a t", a=2)).then_inc(ev_dve, 1)
                for u in range(U):
                    dve.wait_ge(scored, U * b + u + 1)
                    if u < U1:
                        i, h = u // 8, 2 * (u % 8)
                        nc.vector.tensor_reduce(top[:, 0, i, h:h + 2], AB[u % 2][:, :, 0:P * (i + 1)], AX.X, ALU.max).then_inc(maxed, 1)
                    else:
                        h = 2 * (u - U1)
                        nc.vector.tensor_reduce(top[:, 1, :, h:h + 2].rearrange("p i a -> p a i"),
                                                AB[u % 2][:].rearrange("p a (i k) -> p a i k", i=NT), AX.X, ALU.max).then_inc(maxed, 1)
                dve.wait_ge(maxed, U * b + U)
                link(nc.vector.tensor_scalar(ntop[:], top[:], -1.0, None, ALU.mult))
                link(nc.vector.tensor_copy(nparts[:, :, :, :, 0], ntop[:]))
                link(nc.vector.tensor_tensor(nrest[:], ntop[:], nparts[:, :, :, :, 0], ALU.subtract))
                link(nc.vector.tensor_copy(nparts[:, :, :, :, 1], nrest[:]))
                link(nc.vector.tensor_tensor(nrest[:], nrest[:], nparts[:, :, :, :, 1], ALU.subtract))
                nc.vector.tensor_copy(nparts[:, :, :, :, 2], nrest[:]).then_inc(nsplit, 1)
                for g in range(A_KV):
                    dve.wait_ge(pv_done, A_HEADS * b + 4 * g + 4)
                    for a in range(2):
                        nc.vector.tensor_copy(ot[:, a, :], CB[a][:]).then_inc(ot_ready, 1)
                    dve.wait_ge(ot_turned, A_KV * b + g + 1)
                    turned = [TB[a][:].rearrange("p (i h c) -> p i h c", i=NT, h=4) for a in range(2)]
                    for a in range(2):
                        ins = nc.vector.reciprocal(inv_z[:, a, :, :], turned[a][:, :, :, A_D])
                    link(ins)
                    for a in range(2):
                        ins = nc.vector.tensor_tensor(scaled[:, a, :, :, :], turned[a][:, :, :, 0:A_D],
                                                      inv_z[:, a, :, :, None].broadcast_to([P, NT, 4, A_D]), ALU.mult)
                    link(ins)
                    nc.vector.tensor_tensor(mixed[:, :, 4 * g * A_D:4 * (g + 1) * A_D].rearrange("p i (h d) -> p i h d", h=4),
                                            scaled[:, 0, :, :, :], scaled[:, 1, :, :, :], ALU.add).then_inc(normed, 1)
                    dve.wait_ge(normed, A_KV * b + g + 1)
                dve.wait_ge(o_proj, b + 1)
                nc.vector.tensor_tensor(y[:], AB[0][:].rearrange("p a (t c) -> p (a t) c", t=2), x[:], ALU.add).then_inc(resid, 1)
                dve.wait_ge(resid, b + 1)
                for t in range(NT):
                    ins = nc.vector.bn_stats(stats[:, t, :], y[:, t, :])
                link(ins)
                dve.sem_inc(carrier_dve)
                for t in range(NT):
                    ins = nc.vector.bn_aggr(mean_var[:, t, :], stats[:, t, :])
                link(ins)
                dve.wait_ge(rstd_ready, b)
                nc.vector.tensor_scalar(rstd[:], mean_var[:, :, 1], EPS_LN, None, ALU.add).then_inc(var_ready, 1)
                dve.wait_ge(rstd_ready, b + 1)
                dve.wait_ge(stored, 16 * b)
                for t in range(NT):
                    ins = nc.vector.tensor_scalar(x1[:, t, :], y[:, t, :], mean_var[:, t, 0:1], rstd[:, t:t + 1],
                                                  ALU.subtract, ALU.mult)
                ins.then_inc(ln_done, 1)
                dve.wait_ge(ln_done, b + 1)
                assert count[0] == K_CHAIN, count[0]
    nc.clear_and_free_semaphores(sems)
    nc.all_engine_barrier()


F_E, F_H, F_TOP = 8, 128, 2
F_SH = 2 * F_H // P
F_UNITS = F_SH + F_E
F_SUMS = 1 + F_E
SENTINEL = -3.0e38


def layer0_experts(nc, d):
    ctx, sems = ExitStack(), []
    with ctx:
        def sb(name, shape, dt=F32):
            return ctx.enter_context(nc.sbuf_tensor("f_" + name, shape, dt))

        def pb(name, shape, dt=F32):
            return ctx.enter_context(nc.psum_tensor("f_" + name, shape, dt))

        def sem(name):
            sems.append(nc.alloc_semaphore("f_" + name))
            return sems[-1]

        ident = sb("ident", [P, P])
        w_gate = sb("w_gate", [P, CK, F_E])
        w1, w2 = sb("w1", [P, CK, F_UNITS, F_H]), sb("w2", [P, F_UNITS, C])
        b1, b2 = sb("b1", [P, F_UNITS]), sb("b2", [F_E + 1, C])
        x, xT = sb("x", [P, NT, C]), sb("xT", [P, CK, T])
        logits, swapped = sb("logits", [P, NT, F_E + 6]), sb("swapped", [P, NT, F_E + 6])
        best, chosen = sb("best", [P, NT, 8]), sb("chosen", [P, NT, 8])
        weight, mask = sb("weight", [P, NT, F_E]), sb("mask", [P, NT, F_E])
        total = sb("total", [P, NT])
        gates, gatesT = sb("gates", [P, NT, F_E + 1]), sb("gatesT", [F_E + 1, T])
        h = sb("h", [P, 4, T])
        y, x2 = sb("y", [P, NT, C]), sb("x2", [P, NT, C])
        stats, mean_var = sb("stats", [P, NT, 6]), sb("mean_var", [P, NT, 2])
        rstd, mhalf = sb("rstd", [P, NT]), sb("mhalf", [P, NT])

        TB = [pb(f"turn{n}", [P, T]) for n in range(2)]
        HB = [pb(f"hid{n}", [P, T]) for n in range(2)]
        YB = [pb(f"sum{n}", [P, NT, C]) for n in range(2)]

        loaded, x_in, x_turned, xT_ready, consts = sem("loaded"), sem("x_in"), sem("x_turned"), sem("xT_ready"), sem("consts")
        routed, shifted, exped, gated, g_turned, gT_ready = (sem(n) for n in ("routed", "shifted", "exped", "gated", "g_turned", "gT_ready"))
        hidden, gelued, summed, added, chain = (sem(n) for n in ("hidden", "gelued", "summed", "added", "chain"))
        var_ready, rstd_ready, ln_done, stored = (sem(n) for n in ("var_ready", "rstd_ready", "ln_done", "stored"))
        x1_b = d["x1"].rearrange("(b t p) c -> b p t c", p=P, t=NT)
        x2_b = d["x2"].rearrange("(b t p) c -> b p t c", p=P, t=NT)
        k_chain = 10

        carrier, carrier_pool = sem("carrier"), sem("carrier_pool")
        block = ctx.enter_context(nc.Block())

        @block.sync
        def _(sp):
            loads = [(ident[:], d["c_ident"]), (w_gate[:], d["L0_ffn_gate_w"].rearrange("(k p) n -> p k n", p=P)),
                     (b2[0:F_E, :], d["L0_ffn_b2"]), (b2[F_E:F_E + 1, :], d["L0_ffn_shared_b2"].rearrange("(a n) -> a n", a=1)),
                     (w2[:, 0:F_SH, :], d["L0_ffn_shared_w2"].rearrange("(k p) n -> p k n", p=P)),
                     (w2[:, F_SH:, :], d["L0_ffn_w2"].rearrange("e p n -> p e n"))]
            for k in range(CK):
                loads += [(w1[:, k, 0:F_SH, :], d["L0_ffn_shared_w1"][k * P:(k + 1) * P, :].rearrange("p (e n) -> p e n", e=F_SH)),
                          (w1[:, k, F_SH:, :], d["L0_ffn_w1"][:, k * P:(k + 1) * P, :].rearrange("e p n -> p e n"))]
            for dst, src in loads:
                sp.dma_start(dst, src).then_inc(loaded, 16)
            with nc.allow_non_contiguous_dma(reason="biases, one value a partition"):
                sp.dma_start(b1[:, 0:F_SH], d["L0_ffn_shared_b1"].rearrange("(e p) -> p e", p=P)).then_inc(loaded, 16)
                sp.dma_start(b1[:, F_SH:], d["L0_ffn_b1"].rearrange("e p -> p e")).then_inc(loaded, 16)
            with sp.Fori(0, BATCH) as b:
                sp.wait_ge(added, F_SUMS * b)
                sp.dma_start(x[:], x1_b[b, :, :, :]).then_inc(x_in, 16)

        @block.tensor
        def _(pe):
            pe.wait_ge(loaded, 16 * 12)
            with pe.Fori(0, BATCH) as b:
                pe.wait_ge(x_in, 16 * b + 16)
                pe.wait_ge(gT_ready, b)
                for k in range(CK):
                    for t in range(NT):
                        last = nc.tensor.transpose(TB[k][:, t * P:(t + 1) * P], x[:, t, k * P:(k + 1) * P], ident[:])
                last.then_inc(x_turned, 1)
                pe.wait_ge(xT_ready, 2 * b + 2)
                for t in range(NT):
                    for k in range(CK):
                        last = nc.tensor.matmul(TB[0][:, t * F_E:(t + 1) * F_E], xT[:, k, t * P:(t + 1) * P], w_gate[:, k, :],
                                                start=k == 0, stop=k == CK - 1)
                last.then_inc(routed, 1)

                def hide(n):
                    pe.wait_ge(gelued, F_UNITS * b + max(n - 1, 0))
                    for k in range(CK):
                        last = nc.tensor.matmul(HB[n % 2][:], w1[:, k, n, :], xT[:, k, :], start=k == 0, stop=k == CK - 1)
                    last.then_inc(hidden, 1)

                def project(u):
                    chunks = range(F_SH) if u == 0 else [u + F_SH - 1]
                    pe.wait_ge(gelued, F_UNITS * b + chunks[-1] + 1)
                    pe.wait_ge(added, F_SUMS * b + max(u - 1, 0))
                    for t in range(NT):
                        for n in chunks:
                            last = nc.tensor.matmul(YB[u % 2][:, t, :], h[:, n % 4, t * P:(t + 1) * P], w2[:, n, :],
                                                    start=n == chunks[0], stop=u > 0)
                        if u == 0:
                            last = nc.tensor.matmul(YB[0][:, t, :], gatesT[:, t * P:(t + 1) * P], b2[:], start=False, stop=True)
                    last.then_inc(summed, 1)

                for n in range(F_SH + 1):
                    hide(n)
                pe.wait_ge(gated, b + 1)
                for t in range(NT):
                    last = nc.tensor.transpose(TB[1][0:F_E + 1, t * P:(t + 1) * P], gates[:, t, :], ident[:])
                last.then_inc(g_turned, 1)
                pe.wait_ge(gT_ready, b + 1)
                for u in range(F_SUMS):
                    if F_SH + 1 + u < F_UNITS:
                        hide(F_SH + 1 + u)
                    project(u)

        @block.scalar
        def _(act):
            act.wait_ge(loaded, 16 * 12)
            with act.Fori(0, BATCH) as b:
                act.wait_ge(x_turned, b + 1)
                for k in range(CK):
                    nc.scalar.activation(xT[:, k, :], TB[k][:], ACT.Copy).then_inc(xT_ready, 1)
                act.wait_ge(shifted, b + 1)
                nc.scalar.activation(weight[:], weight[:], ACT.Exp).then_inc(exped, 1)
                for n in range(F_UNITS):
                    if n == F_SH + 1:
                        act.wait_ge(g_turned, b + 1)
                        nc.scalar.activation(gatesT[:], TB[1][0:F_E + 1, :], ACT.Copy).then_inc(gT_ready, 1)
                    act.wait_ge(hidden, F_UNITS * b + n + 1)
                    act.wait_ge(summed, F_SUMS * b + (0 if n < 4 else max(n - 4 - F_SH + 2, 1)))
                    nc.scalar.activation(h[:, n % 4, :], HB[n % 2][:], ACT.Gelu, bias=b1[:, n:n + 1]).then_inc(gelued, 1)

        @block.gpsimd
        def _(pool):
            nc.gpsimd.memset(mhalf[:], -0.5).then_inc(consts, 1)
            nc.gpsimd.memset(gates[:], 1.0).then_inc(consts, 1)
            nc.gpsimd.memset(logits[:], SENTINEL).then_inc(consts, 1)
            nc.gpsimd.memset(chosen[:], SENTINEL).then_inc(consts, 1)
            pool.wait_ge(consts, 4)
            with pool.Fori(0, BATCH) as b:
                pool.wait_ge(var_ready, b + 1)
                nc.gpsimd.tensor_tensor(rstd[:], rstd[:], mhalf[:], ALU.pow).then_inc(rstd_ready, 1)
                pool.wait_ge(ln_done, b + 1)
                pool.sem_inc(carrier_pool)
                pool.dma_start(x2_b[b, :, :, :], x2[:]).then_inc(stored, 16)
            pool.wait_ge(stored, 16 * BATCH)

        @block.vector
        def _(dve):
            dve.wait_ge(loaded, 16 * 12)
            dve.wait_ge(consts, 4)
            with dve.Fori(0, BATCH) as b:
                count = [0]

                def link(ins):
                    count[0] += 1
                    ins.then_inc(chain, 1)
                    dve.wait_ge(chain, k_chain * b + count[0])

                dve.wait_ge(routed, b + 1)
                link(nc.vector.tensor_copy(logits[:, :, 0:F_E], TB[0][:, 0:NT * F_E].rearrange("p (t e) -> p t e", t=NT)))
                dve.sem_inc(carrier)
                for t in range(NT):
                    ins = nc.vector.max(best[:, t, :], logits[:, t, 0:F_E])
                link(ins)
                link(nc.vector.tensor_copy(chosen[:, :, 0:F_TOP], best[:, :, 0:F_TOP]))
                nc.vector.tensor_tensor(weight[:], logits[:, :, 0:F_E], best[:, :, 0:1].broadcast_to([P, NT, F_E]),
                                        ALU.subtract).then_inc(shifted, 1)
                for t in range(NT):
                    ins = nc.vector.match_replace(swapped[:, t, :], chosen[:, t, :], logits[:, t, :], -SENTINEL)
                link(ins)
                link(nc.vector.tensor_tensor(mask[:], swapped[:, :, 0:F_E], logits[:, :, 0:F_E], ALU.not_equal))
                dve.wait_ge(exped, b + 1)
                link(nc.vector.tensor_tensor(weight[:], weight[:], mask[:], ALU.mult))
                link(nc.vector.tensor_reduce(total[:], weight[:], AX.X, ALU.add))
                link(nc.vector.reciprocal(total[:], total[:]))
                nc.vector.tensor_tensor(gates[:, :, 0:F_E], weight[:], total[:, :, None].broadcast_to([P, NT, F_E]),
                                        ALU.mult).then_inc(gated, 1)
                dve.wait_ge(gated, b + 1)
                for u in range(F_SUMS):
                    dve.wait_ge(summed, F_SUMS * b + u + 1)
                    if u == 0:
                        ins = nc.vector.tensor_tensor(y[:], YB[0][:], x[:], ALU.add)
                    else:
                        for t in range(NT):
                            ins = nc.vector.scalar_tensor_tensor(y[:, t, :], YB[u % 2][:, t, :], gates[:, t, u - 1:u], y[:, t, :],
                                                                 ALU.mult, ALU.add)
                    ins.then_inc(added, 1)
                    dve.wait_ge(added, F_SUMS * b + u + 1)
                for t in range(NT):
                    ins = nc.vector.bn_stats(stats[:, t, :], y[:, t, :])
                link(ins)
                dve.sem_inc(carrier)
                for t in range(NT):
                    ins = nc.vector.bn_aggr(mean_var[:, t, :], stats[:, t, :])
                link(ins)
                nc.vector.tensor_scalar(rstd[:], mean_var[:, :, 1], EPS_LN, None, ALU.add).then_inc(var_ready, 1)
                dve.wait_ge(rstd_ready, b + 1)
                dve.wait_ge(stored, 16 * b)
                for t in range(NT):
                    ins = nc.vector.tensor_scalar(x2[:, t, :], y[:, t, :], mean_var[:, t, 0:1], rstd[:, t:t + 1],
                                                  ALU.subtract, ALU.mult)
                ins.then_inc(ln_done, 1)
                dve.wait_ge(ln_done, b + 1)
                assert count[0] == k_chain, count[0]
    nc.clear_and_free_semaphores(sems)
    nc.all_engine_barrier()


D_H, D_K, D_V, TAPS = 12, 128, 32, 4
KDIM, VDIM = D_H * D_K, D_H * D_V
VC = VDIM // P
CH = NT
EPS_L2, EPS_RMS = 1e-6, 1e-5
BLK = 16
NB = P // BLK
H = P // 2
SERIES = 7


def delta_constants():
    i = np.arange(P)
    out = {}
    out["c_upto"] = (i[:, None] <= i[None, :]).astype(np.float32)
    out["c_after"] = (i[:, None] > i[None, :]).astype(np.float32)
    out["c_past"] = in_bf16(np.repeat(np.where(i[:, None] <= i[None, :], 0.0, NEG)[:, None, :], CH, 1))
    pair = (i[:, None] // 32 == i[None, :] // 32) & (i[:, None] // BLK > i[None, :] // BLK)
    out["c_pair"] = -np.ascontiguousarray(pair.astype(np.float32))
    return out


def layer1_projections(nc, d):
    ctx, sems = ExitStack(), []
    with ctx:
        def sb(name, shape, dt=F32):
            return ctx.enter_context(nc.sbuf_tensor("p_" + name, shape, dt))

        def pb(name, shape, dt=F32):
            return ctx.enter_context(nc.psum_tensor("p_" + name, shape, dt))

        def sem(name):
            sems.append(nc.alloc_semaphore("p_" + name))
            return sems[-1]

        NG = VDIM + 2 * D_H
        ident = sb("ident", [P, P])
        upto, after, ones = sb("upto", [P, P]), sb("after", [P, P]), sb("ones", [P, P])
        w = sb("w", [P, CK, NG])
        x, xT, hT = sb("x", [P, NT, C]), sb("xT", [P, CK, T]), sb("hT", [P, CK, TILES * P])
        norm_w, gate = sb("norm_w", [P, D_V]), sb("gate", [P, NT, VDIM])
        raw = sb("raw", [P, TILES, 2 * D_H])
        dt_bias, decay_rate = sb("dt_bias", [P, D_H]), sb("decay_rate", [P, D_H])
        beta, g = sb("beta", [P, D_H, TILES]), sb("g", [P, D_H, TILES])
        z, e, s, q, acc = (sb(n, [P, D_H, TILES]) for n in "zesqa")
        decays = sb("decays", [P, 3, D_H, TILES])
        wv, cv_w = sb("wv", [P, CK, P]), sb("cv_w", [P, TAPS])
        conv, vT, v_tok = sb("conv", [P, 2, T]), sb("vT", [P, BATCH, T]), sb("v_tok", [P, TILES, P])
        TB = [pb(f"turn{n}", [P, T]) for n in range(2)]
        GB = [pb(f"gate{n}", [P, T]) for n in range(2)]
        VB = [pb(f"val{n}", [P, T]) for n in range(2)]

        loaded, x_in, x_turned, xT_ready, projected, silued, copied, gated, stored = (
            sem(n) for n in ("loaded", "x_in", "x_turned", "xT_ready", "projected", "silued", "copied", "gated", "stored"))
        chain, achain, summed, decayed, out = (sem(n) for n in ("chain", "achain", "summed", "decayed", "out"))
        w_in, v_proj, v_scaled, v_conv, v_silu, v_turned, v_out, v_stored, hT_ready = (
            sem(n) for n in ("w_in", "v_proj", "v_scaled", "v_conv", "v_silu", "v_turned", "v_out", "v_stored", "hT_ready"))
        g_ready, b_ready, e_ready = sem("g_ready"), sem("b_ready"), sem("e_ready")
        x2_b = d["x2"].rearrange("(b t p) c -> b p t c", p=P, t=NT)
        gate_b = d["gate"].rearrange("(b t p) c -> b p t c", p=P, t=NT)
        v_m = d["v"].rearrange("(t p) (m c) -> m p t c", p=P, c=P)
        wv_m = d["L1_attn_Wv"].rearrange("(k p) (m c) -> m p k c", p=P, c=P)
        cv_m = d["L1_attn_conv_wv"].rearrange("(m p) c -> m p c", p=P)
        ones_set, carrier = sem("ones_set"), sem("carrier")

        block = ctx.enter_context(nc.Block())

        @block.sync
        def _(sp):
            for dst, src in ((ident[:], d["c_ident"]), (upto[:], d["c_upto"]), (after[:], d["c_after"]),
                             (w[:, :, 0:VDIM], d["L1_attn_Wg"].rearrange("(k p) n -> p k n", p=P)),
                             (w[:, :, VDIM:VDIM + D_H], d["L1_attn_Wb"].rearrange("(k p) n -> p k n", p=P)),
                             (w[:, :, VDIM + D_H:], d["L1_attn_Wa"].rearrange("(k p) n -> p k n", p=P)),
                             (norm_w[:], d["L1_attn_norm_w"].rearrange("(a n) -> a n", a=1).broadcast_to([P, D_V])),
                             (dt_bias[:], d["L1_attn_dt_bias"].rearrange("(a n) -> a n", a=1).broadcast_to([P, D_H])),
                             (decay_rate[:], d["L1_attn_A_log"].rearrange("(a n) -> a n", a=1).broadcast_to([P, D_H]))):
                sp.dma_start(dst, src).then_inc(loaded, 16)
            with sp.Fori(0, BATCH) as b:
                sp.wait_ge(x_turned, b)
                sp.dma_start(x[:], x2_b[b, :, :, :]).then_inc(x_in, 16)
            with sp.Fori(0, VC) as m:
                sp.wait_ge(v_conv, BATCH * m)
                sp.dma_start(wv[:], wv_m[m, :, :, :]).then_inc(w_in, 16)
                sp.dma_start(cv_w[:], cv_m[m, :, :]).then_inc(w_in, 16)
            sp.wait_ge(hT_ready, 2 * BATCH)
            sp.dma_start(d["hT"], hT[:]).then_inc(out, 16)
            sp.wait_ge(decayed, 1)
            sp.wait_ge(g_ready, 1)
            sp.wait_ge(b_ready, 1)
            sp.dma_start(d["beta"], beta[:]).then_inc(out, 16)
            sp.dma_start(d["g"], g[:]).then_inc(out, 16)
            sp.dma_start(d["decays"], decays[:]).then_inc(out, 16)
            sp.wait_ge(out, 64)

        @block.tensor
        def _(pe):
            pe.wait_ge(loaded, 16 * 9)
            with pe.Fori(0, BATCH) as b:
                pe.wait_ge(x_in, 16 * b + 16)
                for k in range(CK):
                    for t in range(NT):
                        last = nc.tensor.transpose(TB[k][:, t * P:(t + 1) * P], x[:, t, k * P:(k + 1) * P], ident[:])
                last.then_inc(x_turned, 1)
                for t in range(NT):
                    if t == 0:
                        pe.wait_ge(xT_ready, 2 * b + 2)
                    pe.wait_ge(copied, NT * b + max(t - 1, 0))
                    for k in range(CK):
                        last = nc.tensor.matmul(GB[t % 2][:, 0:NG], xT[:, k, t * P:(t + 1) * P], w[:, k, :],
                                                start=k == 0, stop=k == CK - 1)
                    last.then_inc(projected, 1)
            pe.wait_ge(hT_ready, 2 * BATCH)
            with pe.Fori(0, VC) as m:
                pe.wait_ge(w_in, 32 * m + 32)
                for b in range(BATCH):
                    pe.wait_ge(v_conv, BATCH * m + max(b - 1, 0))
                    for k in range(CK):
                        last = nc.tensor.matmul(VB[b % 2][:], wv[:, k, :], hT[:, k, b * T:(b + 1) * T],
                                                start=k == 0, stop=k == CK - 1)
                    last.then_inc(v_proj, 1)
                for b in range(BATCH):
                    pe.wait_ge(v_silu, BATCH * m + b + 1)
                    pe.wait_ge(v_out, BATCH * m + max(b - 1, 0))
                    for t in range(NT):
                        last = nc.tensor.transpose(TB[b % 2][:, t * P:(t + 1) * P], vT[:, b, t * P:(t + 1) * P], ident[:])
                    last.then_inc(v_turned, 1)
            pe.wait_ge(g_ready, 1)
            pe.wait_ge(ones_set, 1)
            n = D_H * TILES
            for lhsT, bank, at in ((upto, GB[0], 0), (after, GB[0], n), (ones, GB[1], 0)):
                last = nc.tensor.matmul(bank[:, at:at + n], lhsT[:], g[:].rearrange("p h t -> p (h t)"), start=True, stop=True)
            last.then_inc(summed, 1)

        @block.scalar
        def _(act):
            act.wait_ge(loaded, 16 * 9)
            with act.Fori(0, BATCH) as b:
                act.wait_ge(x_turned, b + 1)
                for k in range(CK):
                    nc.scalar.activation(xT[:, k, :], TB[k][:], ACT.Copy).then_inc(xT_ready, 1)
                act.wait_ge(stored, 16 * b)
                for t in range(NT):
                    act.wait_ge(projected, NT * b + t + 1)
                    nc.scalar.activation(gate[:, t, :], GB[t % 2][:, 0:VDIM], ACT.Silu).then_inc(silued, 1)
            with act.Fori(0, VC) as m:
                act.wait_ge(w_in, 32 * m + 32)

                def silu(b):
                    act.wait_ge(v_conv, BATCH * m + b + 1)
                    nc.scalar.activation(vT[:, b, :], conv[:, b % 2, :], ACT.Silu).then_inc(v_silu, 1)

                for b in range(BATCH):
                    act.wait_ge(v_proj, BATCH * m + b + 1)
                    nc.scalar.activation(conv[:, b % 2, :], VB[b % 2][:], ACT.Copy, scale=cv_w[:, TAPS - 1:TAPS]).then_inc(v_scaled, 1)
                    silu(b)
            act.wait_ge(copied, TILES)
            act.wait_ge(gated, BATCH)
            nc.scalar.activation(decay_rate[:], decay_rate[:], ACT.Exp).then_inc(achain, 1)
            nc.scalar.activation(beta[:], raw[:, :, 0:D_H].rearrange("p t h -> p h t"), ACT.Exp, scale=-1.0).then_inc(achain, 1)
            act.wait_ge(e_ready, 1)
            nc.scalar.activation(e[:], e[:], ACT.Exp).then_inc(achain, 1)
            act.wait_ge(summed, 1)
            n = D_H * TILES
            dv = decays[:].rearrange("p a h t -> p a (h t)")
            nc.scalar.activation(dv[:, 0:2, :], GB[0][:, 0:2 * n].rearrange("p (a n) -> p a n", a=2), ACT.Exp).then_inc(achain, 1)
            nc.scalar.activation(dv[:, 2, :], GB[1][:, 0:n], ACT.Exp).then_inc(decayed, 1)

        @block.gpsimd
        def _(pool):
            nc.gpsimd.memset(ones[:], 1.0).then_inc(ones_set, 1)
            with pool.Fori(0, BATCH) as b:
                pool.wait_ge(gated, b + 1)
                pool.sem_inc(carrier)
                pool.dma_start(gate_b[b, :, :, :], gate[:]).then_inc(stored, 16)
            with pool.Fori(0, VC) as m:
                pool.wait_ge(v_out, BATCH * m + BATCH)
                pool.sem_inc(carrier)
                pool.dma_start(v_m[m, :, :, :], v_tok[:]).then_inc(v_stored, 16)
            pool.wait_ge(stored, 16 * BATCH)
            pool.wait_ge(v_stored, 16 * VC)

        @block.vector
        def _(dve):
            dve.wait_ge(loaded, 16 * 9)
            with dve.Fori(0, BATCH) as b:
                for k in range(CK):
                    dve.wait_ge(xT_ready, 2 * b + k + 1)
                    nc.vector.tensor_copy(hT[:, k, :].rearrange("p (b t) -> p b t", b=BATCH)[:, b, :], xT[:, k, :]).then_inc(hT_ready, 1)
                for t in range(NT):
                    dve.wait_ge(silued, NT * b + t + 1)
                    nc.vector.tensor_copy(raw[:].rearrange("p (b t) n -> p b t n", b=BATCH)[:, b, t, :], GB[t % 2][:, VDIM:NG])\
                        .then_inc(copied, 1)
                nw = norm_w[:, None, :].broadcast_to([P, NT * D_H, D_V])
                gv = gate[:].rearrange("p t (h v) -> p (t h) v", v=D_V)
                nc.vector.tensor_tensor(gv, gv, nw, ALU.mult).then_inc(gated, 1)
            with dve.Fori(0, VC) as m:
                dve.wait_ge(v_stored, 16 * m)
                for b in range(BATCH):
                    dve.wait_ge(v_scaled, BATCH * m + b + 1)
                    for j in range(1, TAPS):
                        dst = conv[:, b % 2, j:T]
                        ins = nc.vector.scalar_tensor_tensor(dst, VB[b % 2][:, 0:T - j], cv_w[:, TAPS - 1 - j:TAPS - j], dst, ALU.mult, ALU.add)
                        ins.then_inc(v_conv if j == TAPS - 1 else chain, 1)
                        if j < TAPS - 1:
                            dve.wait_ge(chain, 2 * BATCH * m + 2 * b + j)
                for b in range(BATCH):
                    dve.wait_ge(v_turned, BATCH * m + b + 1)
                    nc.vector.tensor_copy(v_tok[:, b * NT:(b + 1) * NT, :], TB[b % 2][:].rearrange("p (t c) -> p t c", t=NT)).then_inc(v_out, 1)
            count = [2 * BATCH * VC]

            def link(ins):
                count[0] += 1
                ins.then_inc(chain, 1)
                dve.wait_ge(chain, count[0])

            dve.wait_ge(copied, TILES)
            dve.wait_ge(achain, 2)
            link(nc.vector.tensor_scalar(beta[:], beta[:], 1.0, None, ALU.add))
            nc.vector.reciprocal(beta[:], beta[:]).then_inc(b_ready, 1)
            link(nc.vector.tensor_tensor(z[:], raw[:, :, D_H:2 * D_H].rearrange("p t h -> p h t"),
                                         dt_bias[:, :, None].broadcast_to([P, D_H, TILES]), ALU.add))
            link(nc.vector.scalar_tensor_tensor(e[:], z[:], -1.0, z[:], ALU.mult, ALU.min))
            nc.vector.tensor_scalar(acc[:], z[:], 0.0, None, ALU.max).then_inc(e_ready, 1)
            dve.wait_ge(achain, 3)
            link(nc.vector.tensor_scalar(s[:], e[:], 2.0, None, ALU.add))
            link(nc.vector.reciprocal(s[:], s[:]))
            link(nc.vector.tensor_tensor(s[:], s[:], e[:], ALU.mult))
            link(nc.vector.tensor_tensor(q[:], s[:], s[:], ALU.mult))
            link(nc.vector.tensor_scalar(z[:], q[:], 1.0 / (2 * SERIES + 1), None, ALU.mult))
            for n in range(SERIES - 1, 0, -1):
                link(nc.vector.scalar_tensor_tensor(z[:], z[:], 1.0 / (2 * n + 1), q[:], ALU.add, ALU.mult))
            link(nc.vector.scalar_tensor_tensor(z[:], z[:], 1.0, s[:], ALU.add, ALU.mult))
            link(nc.vector.scalar_tensor_tensor(z[:], z[:], 2.0, acc[:], ALU.mult, ALU.add))
            link(nc.vector.tensor_scalar(z[:], z[:], -1.0, None, ALU.mult))
            nc.vector.tensor_tensor(g[:], z[:], decay_rate[:, :, None].broadcast_to([P, D_H, TILES]), ALU.mult).then_inc(g_ready, 1)
    nc.clear_and_free_semaphores(sems)
    nc.all_engine_barrier()


def layer1_delta_rule(nc, d):
    ctx, sems = ExitStack(), []
    with ctx:
        def sb(name, shape, dt=F32):
            return ctx.enter_context(nc.sbuf_tensor("d_" + name, shape, dt))

        def pb(name, shape, dt=F32):
            return ctx.enter_context(nc.psum_tensor("d_" + name, shape, dt))

        def sem(name):
            sems.append(nc.alloc_semaphore("d_" + name))
            return sems[-1]

        ident, identb = sb("ident", [P, P]), sb("identb", [P, P], BF16)
        upto, after, ones1 = sb("upto", [P, P]), sb("after", [P, P]), sb("ones1", [P, 1])
        past, pair = sb("past", [P, CH, P], BF16), sb("pair", [P, P])
        hT = sb("hT", [P, CK, TILES * P])
        decays = sb("decays", [P, 3, D_H, TILES])
        beta, g = sb("beta", [P, D_H, TILES]), sb("g", [P, D_H, TILES])
        power = sb("power", [P, 2, TILES])
        w = sb("w", [P, 2, 2, CK, P])
        cw = sb("cw", [P, 2, 2, TAPS])
        v_h, gate_h = sb("v_h", [P, 2, TILES, D_V]), sb("gate_h", [P, 2, TILES, D_V])
        conv = sb("conv", [P, 2, T])
        kq = sb("kq", [P, 2, 2, BATCH, T])
        squares = sb("squares", [P, 2, 2, T])
        norm2, norm = sb("norm2", [P, 2, TILES]), sb("norm", [P, 2, 2, TILES])
        a = sb("a", [P, 2, TILES])
        g_upto = sb("g_upto", [P, 2, CH, P])
        decay = sb("decay", [P, 2, CH, P])
        AT, qkT = sb("AT", [P, 2, TILES, P]), sb("qkT", [P, 2, TILES, P])
        blk, prod = sb("blk", [P, BLK, BLK]), sb("prod", [P, BLK, BLK])
        inv, invT = sb("inv", [P, BLK, BLK]), sb("invT", [P, BLK, BLK])
        U16, L16 = sb("U16", [P, TILES, P]), sb("L16", [P, TILES, P])
        U, L = sb("U", [P, TILES, P]), sb("L", [P, TILES, P])
        X1, X2, X3 = sb("X1", [P, TILES, P]), sb("X2", [P, TILES, P]), sb("X3", [P, TILES, P])
        k_tok = sb("k_tok", [P, TILES, P])
        R = sb("R", [P, BATCH, D_V])
        S, S_decayed = sb("S", [P, BATCH, D_V]), sb("S_decayed", [P, BATCH, D_V])
        eps, from_S = sb("eps", [P, BATCH, D_V]), sb("from_S", [P, BATCH, D_V])
        o, o2 = sb("o", [P, TILES, D_V]), sb("o2", [P, TILES, D_V])
        mean2 = sb("mean2", [P, TILES])
        mhalf = sb("mhalf", [P, TILES])
        o_out = sb("o_out", [P, TILES, D_V])

        PB = [pb(f"prep{n}", [P, T]) for n in range(2)]
        DB, NB_ = pb("dec", [P, T]), pb("nrm", [P, 2, TILES])
        LB = [pb(f"rec{n}", [P, CH, P]) for n in range(4)]

        (loaded, consts, w_in, v_in, proj, scaled, conved, silued, squared, norms, n_ready, pow_ready, gu_ready,
         diff, decayed, kk, attn, blk_out, blk_in, inverted, inv_out, inv_back, k_turned, k_ready, x1, x1_e, u1, u1_e, x2,
         x2_e, u2, u2_e, x3, x3_e, u3, u3_e, from_s, r_ready, solved, eps_ready, added, s_ready, o_ready, s_dec, mean_ready,
         rms_ready, o_done, stored, chain, bchain, rchain) = (sem(n) for n in (
            "loaded", "consts", "w_in", "v_in", "proj", "scaled", "conved", "silued", "squared", "norms", "n_ready", "pow_ready",
            "gu_ready", "diff", "decayed", "kk", "attn", "blk_out", "blk_in", "inverted", "inv_out",
            "inv_back", "k_turned", "k_ready", "x1", "x1_e", "u1", "u1_e", "x2", "x2_e", "u2", "u2_e", "x3", "x3_e", "u3",
            "u3_e", "from_s", "r_ready", "solved", "eps_ready", "added", "s_ready", "o_ready", "s_dec", "mean_ready",
            "rms_ready", "o_done", "stored", "chain", "bchain", "rchain"))

        carrier, sp_carrier = sem("carrier"), sem("sp_carrier")
        wkq = [d["L1_attn_Wk"].rearrange("(k p) (h c) -> h p k c", p=P, c=P), d["L1_attn_Wq"].rearrange("(k p) (h c) -> h p k c", p=P, c=P)]
        cwkq = [d["L1_attn_conv_wk"].rearrange("(h p) c -> h p c", p=P), d["L1_attn_conv_wq"].rearrange("(h p) c -> h p c", p=P)]
        v_d, gate_d, o_d = (d[n].rearrange("(t p) (h c) -> h p t c", p=P, c=D_V) for n in ("v", "gate", "o"))
        a_blk, u_blk, l_blk = d["a_blk"], d["u_blk"], d["l_blk"]
        by_b = lambda t, c: t.rearrange("p (b c) v -> p b c v", b=BATCH)[:, :, c, :]

        def decays_of(which, n, c):
            return decays[:, which, n, :].rearrange("p (b c) -> p b c", b=BATCH)[:, :, c:c + 1].broadcast_to([P, BATCH, D_V])

        def later(n, least=1):
            return not isinstance(n, int) or n >= least

        def steps(eng, names):
            prepare, recur, invert = names
            prepare(0, 0)
            invert(0, 0)
            with eng.Fori(0, D_H // 2 - 1) as i:
                for s in range(2):
                    prepare(2 * i + s + 1, 1 - s)
                    recur(2 * i + s, s, True)
            prepare(D_H - 1, 1)
            recur(D_H - 2, 0, True)
            recur(D_H - 1, 1, False)

        block = ctx.enter_context(nc.Block())

        @block.sync
        def _(sp):
            for dst, src in ((ident[:], d["c_ident"]), (identb[:], d["c_identb"]), (upto[:], d["c_upto"]), (after[:], d["c_after"]),
                             (past[:], d["c_past"]), (pair[:], d["c_pair"]), (hT[:], d["hT"]), (decays[:], d["decays"]),
                             (beta[:], d["beta"]), (g[:], d["g"])):
                sp.dma_start(dst, src).then_inc(loaded, 16)

            def load_weights(n, s):
                if later(n, 2):
                    sp.wait_ge(conved, 8 * n - 8)
                    sp.sem_inc(sp_carrier)
                for i in range(2):
                    sp.dma_start(w[:, s, i, :, :], wkq[i][n, :, :, :]).then_inc(w_in, 16)
                    sp.dma_start(cw[:, s, i, :], cwkq[i][n, :, :]).then_inc(w_in, 16)

            def prepare(n, s):
                if later(n, 2):
                    sp.wait_ge(o_done, n - 1)
                    sp.sem_inc(sp_carrier)
                sp.dma_start(v_h[:, s, :, :], v_d[n, :, :, :]).then_inc(v_in, 16)
                sp.dma_start(gate_h[:, s, :, :], gate_d[n, :, :, :]).then_inc(v_in, 16)
                sp.wait_ge(attn, 8 * n + 8)
                for j in range(NB):
                    r = slice(BLK * j, BLK * (j + 1))
                    sp.dma_start(a_blk[j, :, :, :].rearrange("c s t -> s c t"), AT[r, s, :, r]).then_inc(blk_out, 16)
                sp.wait_ge(blk_out, 16 * NB * (n + 1))
                sp.sem_inc(sp_carrier)
                if later(n):
                    sp.wait_ge(inverted, 2 * n)
                sp.dma_start(blk[:].rearrange("p s t -> p (s t)"), a_blk.rearrange("j c s t -> (j c) (s t)")).then_inc(blk_in, 16)
                if not isinstance(n, int) or n < D_H - 1:
                    load_weights(n + 1, 1 - s)

            def recur(n, s, follow):
                if follow:
                    invert(n + 1, 1 - s)
                sp.wait_ge(o_done, n + 1)
                sp.sem_inc(sp_carrier)
                sp.dma_start(o_d[n, :, :, :], o_out[:]).then_inc(stored, 16)

            def invert(n, s):
                sp.wait_ge(inverted, 2 * n + 2)
                sp.dma_start(u_blk.rearrange("j c s t -> (j c) (s t)"), inv[:].rearrange("p s t -> p (s t)")).then_inc(inv_out, 16)
                sp.dma_start(l_blk.rearrange("j c s t -> (j c) (s t)"), invT[:].rearrange("p s t -> p (s t)")).then_inc(inv_out, 16)
                sp.wait_ge(inv_out, 32 * n + 32)
                for j in range(NB):
                    r = slice(BLK * j, BLK * (j + 1))
                    sp.dma_start(U16[r, :, r], u_blk[j, :, :, :].rearrange("c s t -> s c t")).then_inc(inv_back, 16)
                    sp.dma_start(L16[r, :, r], l_blk[j, :, :, :].rearrange("c s t -> s c t")).then_inc(inv_back, 16)

            load_weights(0, 0)
            steps(sp, (prepare, recur, invert))
            sp.wait_ge(stored, 16 * D_H)

        @block.tensor
        def _(pe):
            pe.wait_ge(loaded, 160)
            pe.wait_ge(consts, 9)

            def prepare(n, s):
                pe.wait_ge(w_in, 64 * n + 64)

                def sum_squares(b):
                    if b == 0 and later(n):
                        pe.wait_ge(n_ready, n)
                    pe.wait_ge(squared, BATCH * n + b + 1)
                    for i in range(2):
                        for c in range(CH):
                            last = nc.tensor.matmul(NB_[:, i, b * CH + c:b * CH + c + 1], squares[:, b % 2, i, c * P:(c + 1) * P], ones1[:],
                                                    start=True, stop=True)
                    last.then_inc(norms, 1)

                for f in range(8):
                    b, i = f // 2, f % 2
                    if f >= 2:
                        pe.wait_ge(conved, 8 * n + f - 1)
                    elif later(n):
                        pe.wait_ge(attn, 8 * n)
                    for k in range(CK):
                        last = nc.tensor.matmul(PB[f % 2][:], w[:, s, i, k, :], hT[:, k, b * T:(b + 1) * T], start=k == 0, stop=k == CK - 1)
                    last.then_inc(proj, 1)
                    if f in (5, 7):
                        sum_squares(f // 2 - 2)

                def differences(b):
                    pe.wait_ge(gu_ready, BATCH * n + b + 1)
                    if b or later(n):
                        pe.wait_ge(decayed, BATCH * n + b)
                    nc.tensor.matmul(DB[:], after[:], g_upto[:, b % 2, :, :].rearrange("p c t -> p (c t)"), start=True, stop=False)
                    nc.tensor.matmul(DB[:], identb[:], past[:].rearrange("p c t -> p (c t)"), start=False, stop=True).then_inc(diff, 1)

                def products(f):
                    b, c2 = f // 2, f % 2
                    if f < 2:
                        pe.wait_ge(conved, 8 * n + 8)
                        pe.wait_ge(silued, 8 * n + 2)
                    else:
                        pe.wait_ge(attn, 8 * n + f - 1)
                    for c in range(2):
                        t0 = (2 * c2 + c) * P
                        last = nc.tensor.matmul(PB[f % 2][:, 2 * c * P:2 * (c + 1) * P], kq[:, s, 0, b, t0:t0 + P], kq[:, s, :, b, t0:t0 + P],
                                                start=True, stop=True)
                    last.then_inc(kk, 1)

                differences(0)
                products(0)
                products(1)
                sum_squares(2)
                sum_squares(3)
                for b in range(1, BATCH):
                    differences(b)
                    products(2 * b)
                    products(2 * b + 1)

            def recur(n, s, follow):
                if later(n):
                    pe.wait_ge(o_ready, CH * n)
                for b in range(BATCH):
                    for c in range(CH):
                        last = nc.tensor.transpose(LB[b][:, c, :], kq[:, s, 0, b, c * P:(c + 1) * P], ident[:])
                    last.then_inc(k_turned, 1)
                pe.wait_ge(inv_back, 16 * 2 * NB * (n + 1))
                def times(b, left, right):
                    for c in range(CH):
                        last = nc.tensor.matmul(LB[b][:, c, :], left[:, b * CH + c, :], right[:, b * CH + c, :], start=True, stop=True)
                    return last

                A = AT[:, s, :, :]
                for b in range(BATCH):
                    pe.wait_ge(k_ready, BATCH * n + b + 1)
                    times(b, A, L16).then_inc(x1, 1)
                for b in range(BATCH):
                    pe.wait_ge(x1_e, BATCH * n + b + 1)
                    times(b, U16, X1).then_inc(u1, 1)
                for b in range(BATCH):
                    pe.wait_ge(u1_e, 2 * BATCH * n + b + 1)
                    times(b, X1, U16).then_inc(u1, 1)
                for b in range(BATCH):
                    pe.wait_ge(u1_e, 2 * BATCH * n + BATCH + b + 1)
                    times(b, A, L).then_inc(x2, 1)
                for b in range(BATCH):
                    pe.wait_ge(x2_e, BATCH * n + b + 1)
                    times(b, U, X2).then_inc(u2, 1)
                for b in range(BATCH):
                    pe.wait_ge(u2_e, 2 * BATCH * n + b + 1)
                    times(b, X2, U).then_inc(u2, 1)
                for b in range(BATCH):
                    pe.wait_ge(u2_e, 2 * BATCH * n + BATCH + b + 1)
                    pe.sem_inc(carrier)
                    for c in range(CH):
                        last = nc.tensor.matmul(LB[b][H:P, c, 0:H], AT[0:H, s, b * CH + c, H:P], L[0:H, b * CH + c, 0:H], start=True, stop=True)
                    last.then_inc(x3, 1)
                for b in range(BATCH):
                    pe.wait_ge(x3_e, BATCH * n + b + 1)
                    pe.sem_inc(carrier)
                    for c in range(CH):
                        last = nc.tensor.matmul(LB[b][0:H, c, H:P], X3[H:P, b * CH + c, 0:H], U[H:P, b * CH + c, H:P], start=True, stop=True)
                    last.then_inc(u3, 1)
                pe.wait_ge(u3_e, BATCH * (n + 1))
                for c in range(CH):
                    if c:
                        pe.wait_ge(s_ready, (CH - 1) * n + c)
                        for b in range(BATCH):
                            for i in range(2):
                                last = nc.tensor.matmul(LB[0][:, b, i * D_V:(i + 1) * D_V], kq[:, s, i, b, c * P:(c + 1) * P], S[:, b, :],
                                                        start=True, stop=True)
                        last.then_inc(from_s, 1)
                    pe.wait_ge(r_ready, CH * n + c + 1)
                    for b in range(BATCH):
                        last = nc.tensor.matmul(LB[1][:, b, 0:D_V], U[:, b * CH + c, :], R[:, b, :], start=True, stop=True)
                    last.then_inc(solved, 1)
                    pe.wait_ge(eps_ready, CH * n + c + 1)
                    if c < CH - 1:
                        for b in range(BATCH):
                            last = nc.tensor.matmul(LB[3][:, b, 0:D_V], k_tok[:, b * CH + c, :], eps[:, b, :], start=True, stop=True)
                        last.then_inc(added, 1)
                    if c:
                        pe.wait_ge(o_ready, CH * n + c)
                    for b in range(BATCH):
                        last = nc.tensor.matmul(LB[2][:, b, 0:D_V], qkT[:, s, b * CH + c, :], eps[:, b, :], start=True, stop=True)
                    last.then_inc(added, 1)

            steps(pe, (prepare, recur, lambda n, s: None))

        @block.scalar
        def _(act):
            act.wait_ge(loaded, 160)
            act.wait_ge(consts, 9)

            def prepare(n, s):
                act.wait_ge(w_in, 64 * n + 64)

                def silu(f):
                    b, i = f // 2, f % 2
                    act.wait_ge(conved, 8 * n + f + 1)
                    nc.scalar.activation(kq[:, s, i, b, :], conv[:, f % 2, :], ACT.Silu).then_inc(silued, 1)

                for f in range(8):
                    act.wait_ge(proj, 8 * n + f + 1)
                    if f >= 2:
                        silu(f - 2)
                        act.wait_ge(silued, 8 * n + f - 1)
                    nc.scalar.activation(conv[:, f % 2, :], PB[f % 2][:], ACT.Copy, scale=cw[:, s, f % 2, TAPS - 1:TAPS]).then_inc(scaled, 1)
                silu(6)
                silu(7)
                for b in range(BATCH):
                    act.wait_ge(diff, BATCH * n + b + 1)
                    if b >= 2:
                        act.wait_ge(attn, 8 * n + 2 * b - 2)
                    nc.scalar.activation(decay[:, b % 2, :, :], DB[:].rearrange("p (c t) -> p c t", c=CH), ACT.Exp).then_inc(decayed, 1)

            def recur(n, s, follow):
                def cut(dst, src, r, c, done=None, sign=1.0):
                    ins = nc.scalar.activation(dst[r, :, c], src[r, :, c], ACT.Copy, scale=sign)
                    if done:
                        ins.then_inc(done, 1)

                q = [slice(32 * j, 32 * (j + 1)) for j in range(4)]
                lo, hi = slice(0, H), slice(H, P)
                rows = [slice(b * CH, (b + 1) * CH) for b in range(BATCH)]
                for b in range(BATCH):
                    act.wait_ge(x2, BATCH * n + b + 1)
                    cut(X2[:, rows[b], :], LB[b], q[1], q[0], sign=-1.0)
                    cut(X2[:, rows[b], :], LB[b], q[3], q[2], x2_e, sign=-1.0)
                for b in range(BATCH):
                    act.wait_ge(u2, 2 * BATCH * n + b + 1)
                    cut(L[:, rows[b], :], LB[b], q[1], q[0], u2_e)
                for b in range(BATCH):
                    act.wait_ge(u2, 2 * BATCH * n + BATCH + b + 1)
                    cut(U[:, rows[b], :], LB[b], q[0], q[1])
                    cut(U[:, rows[b], :], LB[b], q[2], q[3], u2_e)
                for b in range(BATCH):
                    act.wait_ge(x3, BATCH * n + b + 1)
                    cut(X3[:, rows[b], :], LB[b], hi, lo, x3_e, sign=-1.0)
                for b in range(BATCH):
                    act.wait_ge(u3, BATCH * n + b + 1)
                    cut(U[:, rows[b], :], LB[b], lo, hi, u3_e)

            steps(act, (prepare, recur, lambda n, s: None))

        @block.gpsimd
        def _(pool):
            for m, value in ((U16, 0.0), (L16, 0.0), (X2, 0.0), (X3, 0.0), (inv, 0.0), (ones1, 1.0), (mhalf, -0.5)):
                nc.gpsimd.memset(m[:], value).then_inc(consts, 1)
            nc.gpsimd.memset(power[:, 0, :], 0.5)
            nc.gpsimd.memset(power[:, 1, :], -0.5).then_inc(consts, 1)
            pool.wait_ge(consts, 8)
            nc.gpsimd.affine_select(out=inv[:], in_=inv[:], compare_op=ALU.not_equal, fill=1.0, base=0,
                                    pattern=[[1, BLK], [-1, BLK]], channel_multiplier=0).then_inc(consts, 1)
            pool.wait_ge(loaded, 160)

            def spread(n, b):
                nc.gpsimd.tensor_tensor(g_upto[:, b % 2, :, :], upto[:, None, :].broadcast_to([P, CH, P]),
                                        g[:, n, b * CH:(b + 1) * CH, None].broadcast_to([P, CH, P]), ALU.mult).then_inc(gu_ready, 1)

            def prepare(n, s):
                for b in range(2):
                    if later(n):
                        pool.wait_ge(diff, BATCH * n - BATCH + b + 3)
                    spread(n, b)
                for b in range(BATCH):
                    pool.wait_ge(silued, 8 * n + 2 * b + 2)
                    if b >= 2:
                        pool.wait_ge(norms, BATCH * n + b - 1)
                    elif later(n):
                        pool.wait_ge(norms, BATCH * n - BATCH + b + 3)
                    src = kq[:, s, :, b, :]
                    nc.gpsimd.tensor_tensor(squares[:, b % 2, :, :], src, src, ALU.mult).then_inc(squared, 1)
                pool.wait_ge(n_ready, n + 1)
                nc.gpsimd.tensor_tensor(norm[:, s, :, :], norm2[:], power[:], ALU.pow).then_inc(pow_ready, 1)
                for b in range(2, BATCH):
                    pool.wait_ge(diff, BATCH * n + b - 1)
                    spread(n, b)

            def recur(n, s, follow):
                for c in range(1, CH):
                    if c < CH - 1:
                        pool.wait_ge(s_ready, (CH - 1) * n + c)
                        nc.gpsimd.tensor_tensor(S_decayed[:], S[:], decays_of(2, n, c), ALU.mult).then_inc(s_dec, 1)
                pool.wait_ge(mean_ready, n + 1)
                nc.gpsimd.tensor_tensor(mean2[:], mean2[:], mhalf[:], ALU.pow).then_inc(rms_ready, 1)

            steps(pool, (prepare, recur, lambda n, s: None))

        @block.vector
        def _(dve):
            dve.wait_ge(loaded, 160)
            dve.wait_ge(consts, 9)

            def prepare(n, s):
                for f in range(8):
                    dve.wait_ge(scaled, 8 * n + f + 1)
                    for j in range(1, TAPS):
                        dst = conv[:, f % 2, j:T]
                        ins = nc.vector.scalar_tensor_tensor(dst, PB[f % 2][:, 0:T - j], cw[:, s, f % 2, TAPS - 1 - j:TAPS - j], dst, ALU.mult, ALU.add)
                        if j < TAPS - 1:
                            ins.then_inc(chain, 1)
                            dve.wait_ge(chain, 19 * n + 2 * f + j)
                    ins.then_inc(conved, 1)
                dve.wait_ge(norms, BATCH * (n + 1))
                if later(n):
                    dve.wait_ge(pow_ready, n)
                nc.vector.tensor_scalar(norm2[:], NB_[:], EPS_L2, None, ALU.add).then_inc(n_ready, 1)
                dve.wait_ge(n_ready, n + 1)
                nc.vector.reciprocal(a[:, s, :], norm2[:, 0, :]).then_inc(chain, 1)
                dve.wait_ge(chain, 19 * n + 17)
                nc.vector.tensor_tensor(a[:, s, :], a[:, s, :], beta[:, n, :], ALU.mult).then_inc(chain, 1)
                dve.wait_ge(chain, 19 * n + 18)
                for f in range(8):
                    b, c2 = f // 2, f % 2
                    if c2 == 0:
                        dve.wait_ge(decayed, BATCH * n + b + 1)
                    dve.wait_ge(kk, 8 * n + f + 1)
                    bank = PB[f % 2][:].rearrange("p (c i t) -> p c i t", c=2, i=2)
                    for c in range(2):
                        t = b * CH + 2 * c2 + c
                        nc.vector.scalar_tensor_tensor(AT[:, s, t, :], bank[:, c, 0, :], a[:, s, t:t + 1], decay[:, b % 2, 2 * c2 + c, :], ALU.mult, ALU.mult)
                    t = b * CH + 2 * c2
                    nc.vector.tensor_tensor(qkT[:, s, t:t + 2, :], bank[:, :, 1, :], decay[:, b % 2, 2 * c2:2 * c2 + 2, :], ALU.mult).then_inc(attn, 1)
                dve.wait_ge(pow_ready, n + 1)
                dve.wait_ge(v_in, 32 * n + 32)
                nc.vector.tensor_tensor(v_h[:, s, :, :], v_h[:, s, :, :], norm[:, s, 0, :, None].broadcast_to([P, TILES, D_V]), ALU.mult)\
                    .then_inc(chain, 1)
                dve.wait_ge(chain, 19 * n + 19)

            def invert_rows(n):
                dve.wait_ge(blk_in, 16 * n + 16)
                if later(n):
                    dve.wait_ge(inv_out, 32 * n)
                for m in range(1, BLK):
                    r = BLK - 1 - m
                    left = blk[:, r, None, r + 1:BLK].broadcast_to([P, m, m])
                    right = inv[:, r + 1:BLK, r + 1:BLK].rearrange("p t c -> p c t")
                    nc.vector.tensor_tensor(prod[:, 0:m, 0:m], left, right, ALU.mult).then_inc(bchain, 1)
                    dve.wait_ge(bchain, (2 * BLK - 3) * n + 2 * m - 1)
                    ins = nc.vector.tensor_reduce(inv[:, r, r + 1:BLK], prod[:, 0:m, 0:m], AX.X, ALU.add, negate=True)
                    if r:
                        ins.then_inc(bchain, 1)
                        dve.wait_ge(bchain, (2 * BLK - 3) * n + 2 * m)
                ins.then_inc(inverted, 1)
                dve.wait_ge(inverted, 2 * n + 1)
                nc.vector.tensor_copy(invT[:].rearrange("p t s -> p s t"), inv[:]).then_inc(inverted, 1)

            def recur(n, s, follow):
                rows = [slice(b * CH, (b + 1) * CH) for b in range(BATCH)]
                for b in range(BATCH):
                    dve.wait_ge(k_turned, BATCH * n + b + 1)
                    dec = decays[:, 1, n, b * CH:(b + 1) * CH]
                    nc.vector.tensor_tensor(k_tok[:, rows[b], :], LB[b][:], dec[:, :, None].broadcast_to([P, CH, P]), ALU.mult).then_inc(k_ready, 1)
                for b in range(BATCH):
                    dve.wait_ge(x1, BATCH * n + b + 1)
                    nc.vector.tensor_tensor(X1[:, rows[b], :], LB[b][:], pair[:, None, :].broadcast_to([P, CH, P]), ALU.mult).then_inc(x1_e, 1)
                for b in range(BATCH):
                    dve.wait_ge(u1, 2 * BATCH * n + b + 1)
                    nc.vector.tensor_tensor(L[:, rows[b], :], LB[b][:], L16[:, rows[b], :], ALU.add).then_inc(u1_e, 1)
                for b in range(BATCH):
                    dve.wait_ge(u1, 2 * BATCH * n + BATCH + b + 1)
                    nc.vector.tensor_tensor(U[:, rows[b], :], LB[b][:], U16[:, rows[b], :], ALU.add).then_inc(u1_e, 1)
                base = 7 * n
                if follow:
                    invert_rows(n + 1)
                for c in range(CH):
                    r_src = by_b(v_h[:, s, :, :], c)
                    if c:
                        dve.wait_ge(o_ready, CH * n + c)
                        dve.wait_ge(from_s, (CH - 1) * n + c)
                        nc.vector.tensor_tensor(from_S[:], LB[0][:, :, D_V:2 * D_V], decays_of(0, n, c), ALU.mult)
                        nc.vector.tensor_tensor(R[:], LB[0][:, :, 0:D_V], decays_of(0, n, c), ALU.mult).then_inc(rchain, 1)
                        dve.wait_ge(rchain, base + c)
                        nc.vector.tensor_tensor(R[:], r_src, R[:], ALU.subtract).then_inc(r_ready, 1)
                    else:
                        nc.vector.tensor_copy(R[:], r_src).then_inc(r_ready, 1)
                    dve.wait_ge(solved, CH * n + c + 1)
                    nc.vector.tensor_tensor(eps[:], LB[1][:, :, 0:D_V], a[:, s, :].rearrange("p (b c) -> p b c", b=BATCH)[:, :, c:c + 1]
                                            .broadcast_to([P, BATCH, D_V]), ALU.mult).then_inc(eps_ready, 1)
                    if c < CH - 1:
                        dve.wait_ge(added, (2 * CH - 1) * n + 2 * c + 1)
                        if c:
                            dve.wait_ge(s_dec, (CH - 2) * n + c)
                            nc.vector.tensor_tensor(S[:], LB[3][:, :, 0:D_V], S_decayed[:], ALU.add).then_inc(s_ready, 1)
                        else:
                            nc.vector.tensor_copy(S[:], LB[3][:, :, 0:D_V]).then_inc(s_ready, 1)
                        dve.wait_ge(added, (2 * CH - 1) * n + 2 * c + 2)
                    else:
                        dve.wait_ge(added, (2 * CH - 1) * n + 2 * c + 1)
                    if c:
                        nc.vector.tensor_tensor(by_b(o[:], c), LB[2][:, :, 0:D_V], from_S[:], ALU.add).then_inc(o_ready, 1)
                    else:
                        nc.vector.tensor_copy(by_b(o[:], c), LB[2][:, :, 0:D_V]).then_inc(o_ready, 1)
                dve.wait_ge(o_ready, CH * n + CH)
                vec = lambda t: t[:, :, None].broadcast_to([P, TILES, D_V])
                nc.vector.tensor_tensor(o[:], o[:], vec(norm[:, s, 1, :]), ALU.mult).then_inc(rchain, 1)
                dve.wait_ge(rchain, base + 4)
                nc.vector.tensor_tensor(o2[:], o[:], o[:], ALU.mult).then_inc(rchain, 1)
                dve.wait_ge(rchain, base + 5)
                nc.vector.tensor_reduce(mean2[:], o2[:], AX.X, ALU.add).then_inc(rchain, 1)
                dve.wait_ge(rchain, base + 6)
                nc.vector.tensor_scalar(mean2[:], mean2[:], 1.0 / D_V, EPS_RMS, ALU.mult, ALU.add).then_inc(mean_ready, 1)
                nc.vector.tensor_tensor(o[:], o[:], gate_h[:, s, :, :], ALU.mult).then_inc(rchain, 1)
                dve.wait_ge(rchain, base + 7)
                dve.wait_ge(rms_ready, n + 1)
                if later(n):
                    dve.wait_ge(stored, 16 * n)
                nc.vector.tensor_tensor(o_out[:], o[:], vec(mean2), ALU.mult).then_inc(o_done, 1)

            steps(dve, (prepare, recur, lambda n, s: invert_rows(n)))
    nc.clear_and_free_semaphores(sems)
    nc.all_engine_barrier()


M_E, M_TOP, M_I, M_IS, CAP = 16, 4, 176, 352, 128
M_C = -(-M_I // P)
M_CS = -(-M_IS // P)
SLOT = 6
TOKENS = BATCH * T
ML_CHAIN = 2 + 1 + 1 + 3 + 4 + (NT - 1) + 4 + 5


def expert_constants():
    i = np.arange(P)
    out = {}
    out["c_before"] = in_bf16(i[:, None] < i[None, :])
    out["c_ones"] = in_bf16(np.ones((P, P)))
    out["c_count"] = in_bf16(np.broadcast_to(i[None, :] + 1.0, (P, P)))
    look = np.zeros((P, M_E, TILES, SLOT))
    look[..., 0] = 1.0
    look[..., 1] = i[:, None, None]
    look[..., 2] = np.arange(TILES)[None, None, :]
    out["c_look"] = in_bf16(look)
    out["c_spare"] = -(TOKENS + i[:, None] + np.zeros((1, M_E))).astype(np.float32)
    return out


def layer1_output(nc, d):
    ctx, sems = ExitStack(), []
    with ctx:
        def sb(name, shape, dt=F32):
            return ctx.enter_context(nc.sbuf_tensor("m_" + name, shape, dt))

        def pb(name, shape, dt=F32):
            return ctx.enter_context(nc.psum_tensor("m_" + name, shape, dt))

        def sem(name):
            sems.append(nc.alloc_semaphore("m_" + name))
            return sems[-1]

        ident, before, ones = sb("ident", [P, P]), sb("before", [P, P], BF16), sb("ones", [P, P], BF16)
        count, spare = sb("count", [P, P], BF16), sb("spare", [P, M_E])
        look = sb("look", [P, M_E, TILES, SLOT], BF16)
        w_o, w_route = sb("w_o", [P, VC, C]), sb("w_route", [P, CK, M_E])
        w_s, w_sd = sb("w_s", [P, CK, 2, M_CS * P]), sb("w_sd", [P, M_CS, C])
        o, x2 = sb("o", [P, NT, VDIM]), sb("x2", [P, NT, C])
        oT = sb("oT", [P, VC, T])
        y, x3, x3T = sb("y", [P, NT, C]), sb("x3", [P, NT, C]), sb("x3T", [P, CK, T])
        act_s, hid_s = sb("act_s", [P, 2, T]), sb("hid_s", [P, M_CS, T])
        y_out = sb("y_out", [P, NT, C])
        stats, mean_var = sb("stats", [P, NT, 6]), sb("mean_var", [P, NT, 2])
        rstd, mhalf = sb("rstd", [P, NT]), sb("mhalf", [P, NT])
        top, probs, total = sb("top", [P, NT]), sb("probs", [P, NT, M_E]), sb("total", [P, NT])
        width = M_E + 8 - M_TOP
        scores, swapped = sb("scores", [P, NT, width]), sb("swapped", [P, NT, width])
        best, chosen = sb("best", [P, NT, 8]), sb("chosen", [P, NT, 8])
        mask, seen = sb("mask", [P, NT, M_E], BF16), sb("seen", [P, NT + 1, M_E], BF16)
        weight, rest = sb("weight", [P, NT, M_E]), sb("rest", [P, NT, M_E])
        rank = sb("rank", [P, M_E, TILES], BF16)
        zeros = sb("zeros", [P, C])
        onehot = sb("onehot", [P, 2, TILES, P], BF16)
        row, row2, w_slot = sb("row", [P, M_E]), sb("row2", [P, M_E]), sb("w_slot", [P, M_E, 1])
        rows = sb("rows", [P, M_E, 1], mybir.dt.uint32)
        g_row, s_row = sb("g_row", [P, 2], mybir.dt.uint32), sb("s_row", [P, 2], mybir.dt.uint32)
        w_e, w_ed = sb("w_e", [P, 2, CK, 2, M_C * P]), sb("w_ed", [P, 2, M_C, C])
        xg, xgT = sb("xg", [P, 2, C]), sb("xgT", [P, 2, CK, P])
        act_e, hid_e = sb("act_e", [P, 2, M_C * P]), sb("hid_e", [P, 2, M_C * P])
        out_e = sb("out_e", [P, 2, C])
        y_in, final = sb("y_in", [P, 2, NT, C]), sb("final", [P, 2, NT, C])

        TB = [pb(f"turn{n}", [P, T]) for n in range(2)]
        GB = [pb(f"hid{n}", [P, T]) for n in range(4)]
        YB = [pb(f"sum{n}", [P, 2, C]) for n in range(2)]

        (loaded, consts, o_in, x2_in, o_turned, oT_ready, projected, resid, chain, var_ready, rstd_ready, ln_done, x3_stored,
         x3_turned, x3T_ready, routed, shifted, exped, masked, ranked, noted, hidden, silued, gated, downed, out_ready, y_stored,
         pads) = (sem(n) for n in (
             "loaded", "consts", "o_in", "x2_in", "o_turned", "oT_ready", "projected", "resid", "chain", "var_ready", "rstd_ready",
             "ln_done", "x3_stored", "x3_turned", "x3T_ready", "routed", "shifted", "exped", "masked", "ranked", "noted", "hidden",
             "silued", "gated", "downed", "out_ready", "y_stored", "pads"))
        (hot, looked, row_ready, g_named, scattered, xg_turned, xgT_ready, e_hidden, e_silued, e_gated,
         e_downed, e_scaled) = (sem("e_" + n) for n in (
             "hot", "looked", "row_ready", "g_named", "scattered", "xg_turned", "xgT_ready",
             "hidden", "silued", "gated", "downed", "scaled"))
        f_chain, f_var, f_rstd, f_done = (sem("f_" + n) for n in ("chain", "var", "rstd", "done"))
        f_in, f_stored = ([sem(f"f_{n}{s}") for s in range(2)] for n in ("in", "stored"))
        w_in = [sem(f"e_w_in{s}") for s in range(2)]
        gathered = [sem(f"e_gathered{s}") for s in range(2)]
        carrier_pool, carrier_dve = sem("carrier_pool"), sem("carrier_dve")

        o_b = d["o"].rearrange("(b t p) c -> b p t c", p=P, t=NT)
        x2_b = d["x2"].rearrange("(b t p) c -> b p t c", p=P, t=NT)
        x3_b = d["x3"][0:TOKENS, :].rearrange("(b t p) c -> b p t c", p=P, t=NT)
        y_b = d["y"][0:TOKENS, :].rearrange("(b t p) c -> b p t c", p=P, t=NT)
        final_b = d["out"].rearrange("(b t p) c -> b p t c", p=P, t=NT)
        LOADED = 16 * 15

        def later(n, least=1):
            return not isinstance(n, int) or n >= least

        def skewed(eng, first, body):
            first()
            with eng.Fori(0, BATCH - 1) as b:
                body(b, True)
            body(BATCH - 1, False)

        block = ctx.enter_context(nc.Block())

        @block.sync
        def _(sp):
            for dst, src in ((ident[:], d["c_ident"]), (w_o[:], d["L1_attn_Wo"].rearrange("(k p) n -> p k n", p=P))):
                sp.dma_start(dst, src).then_inc(loaded, 16)
            with sp.Fori(0, BATCH) as b:
                sp.wait_ge(o_turned, b)
                sp.dma_start(o[:], o_b[b, :, :, :]).then_inc(o_in, 16)
                sp.wait_ge(resid, b)
                sp.dma_start(x2[:], x2_b[b, :, :, :]).then_inc(x2_in, 16)

            def experts(e, s):
                if later(e, 2):
                    sp.wait_ge(e_hidden, e - 1)
                for i, name in ((0, "L1_ffn_w_gate"), (1, "L1_ffn_w_up")):
                    sp.dma_start(w_e[:, s, :, i, 0:M_I], d[name].rearrange("e (k p) n -> e p k n", p=P)[e, :, :, :]).then_inc(w_in[s], 16)
                if later(e, 2):
                    sp.wait_ge(e_downed, e - 1)
                w_down = d["L1_ffn_w_down"]
                sp.dma_start(w_ed[:, s, 0, :], w_down[e, 0:P, :]).then_inc(w_in[s], 16)
                sp.dma_start(w_ed[0:M_I - P, s, 1, :], w_down[e, P:M_I, :]).then_inc(w_in[s], 16)

            sp.wait_ge(consts, 8)
            experts(0, 0)
            experts(1, 1)
            with sp.Fori(0, M_E // 2 - 1) as i:
                for s in range(2):
                    experts(2 * i + s + 2, s)
            sp.wait_ge(scattered, 16 * M_E)
            with sp.Fori(0, BATCH // 2) as i:
                for s in range(2):
                    b = 2 * i + s
                    if s == 0:
                        sp.wait_ge(f_done, b)
                    sp.dma_start(y_in[:, s, :, :], y_b[b, :, :, :]).then_inc(f_in[s], 16)
                for s in range(2):
                    b = 2 * i + s
                    sp.wait_ge(f_done, b + 1)
                    sp.dma_start(final_b[b, :, :, :], final[:, s, :, :]).then_inc(f_stored[s], 16)
            for s in range(2):
                sp.wait_ge(f_stored[s], 16 * BATCH // 2)

        @block.tensor
        def _(pe):
            pe.wait_ge(loaded, LOADED)
            pe.wait_ge(consts, 8)

            def project(b):
                pe.wait_ge(o_in, 16 * b + 16)
                if later(b):
                    pe.wait_ge(noted, b)
                    pe.wait_ge(gated, M_CS * b)
                for k in range(VC):
                    bank = (TB[0], TB[1], GB[0])[k]
                    for t in range(NT):
                        last = nc.tensor.transpose(bank[:, t * P:(t + 1) * P], o[:, t, k * P:(k + 1) * P], ident[:])
                last.then_inc(o_turned, 1)
                pe.wait_ge(oT_ready, VC * b + VC)
                if later(b, 2):
                    pe.wait_ge(out_ready, b - 1)
                for t in range(NT):
                    for k in range(VC):
                        last = nc.tensor.matmul(YB[t // 2][:, t % 2, :], oT[:, k, t * P:(t + 1) * P], w_o[:, k, :], start=k == 0, stop=k == VC - 1)
                last.then_inc(projected, 1)

            def body(b, ahead):
                pe.wait_ge(ln_done, b + 1)
                for k in range(CK):
                    for t in range(NT):
                        last = nc.tensor.transpose(TB[k][:, t * P:(t + 1) * P], x3[:, t, k * P:(k + 1) * P], ident[:])
                last.then_inc(x3_turned, 1)
                pe.wait_ge(x3T_ready, CK * (b + 1))
                for t in range(NT):
                    for k in range(CK):
                        last = nc.tensor.matmul(TB[0][:, t * M_E:(t + 1) * M_E], x3T[:, k, t * P:(t + 1) * P], w_route[:, k, :],
                                                start=k == 0, stop=k == CK - 1)
                last.then_inc(routed, 1)
                for j in range(M_CS):
                    if j == 2:
                        pe.wait_ge(masked, b + 1)
                        for t in range(NT):
                            nc.tensor.matmul(TB[1][:, t * M_E:(t + 1) * M_E], before[:], mask[:, t, :], start=True, stop=False)
                            last = nc.tensor.matmul(TB[1][:, t * M_E:(t + 1) * M_E], ones[:], seen[:, t, :], start=False, stop=True)
                        last.then_inc(ranked, 1)
                        pe.wait_ge(gated, M_CS * b + 1)
                    for i in range(2):
                        for k in range(CK):
                            last = nc.tensor.matmul(GB[2 * (j % 2) + i][:], w_s[:, k, i, j * P:(j + 1) * P], x3T[:, k, :],
                                                    start=k == 0, stop=k == CK - 1)
                    last.then_inc(hidden, 1)
                if ahead:
                    project(b + 1)
                    pe.wait_ge(resid, b + 2)
                pe.wait_ge(gated, M_CS * (b + 1))
                for t in range(NT):
                    for j in range(M_CS):
                        last = nc.tensor.matmul(YB[t // 2][:, t % 2, :], hid_s[:, j, t * P:(t + 1) * P], w_sd[:, j, :],
                                                start=j == 0, stop=j == M_CS - 1)
                last.then_inc(downed, 1)

            skewed(pe, lambda: project(0), body)
            pe.wait_ge(out_ready, BATCH)
            pe.wait_ge(noted, BATCH)
            with pe.Fori(0, M_E // 2) as i:
                for s in range(2):
                    e = 2 * i + s
                    pe.wait_ge(hot, e + 1)
                    for t in range(TILES):
                        last = nc.tensor.matmul(YB[0][:].rearrange("p a (e s) -> p (a e) s", s=8)[:, e, 0:SLOT], onehot[:, s, t, :], look[:, e, t, :],
                                                start=t == 0, stop=t == TILES - 1)
                    last.then_inc(looked, 1)

            with pe.Fori(0, M_E // 2) as i:
                for s in range(2):
                    e = 2 * i + s
                    pe.wait_ge(xgT_ready, e)
                    pe.wait_ge(gathered[s], 16 * i + 16)
                    for k in range(CK):
                        last = nc.tensor.transpose(TB[s][:, k * P:(k + 1) * P], xg[:, s, k * P:(k + 1) * P], ident[:])
                    last.then_inc(xg_turned, 1)
                    pe.wait_ge(w_in[s], 64 * i + 64)
                    pe.wait_ge(xgT_ready, e + 1)
                    pe.wait_ge(e_gated, e)
                    for m in range(2):
                        for j in range(M_C):
                            for k in range(CK):
                                last = nc.tensor.matmul(GB[s][:, (m * M_C + j) * P:(m * M_C + j + 1) * P], w_e[:, s, k, m, j * P:(j + 1) * P],
                                                        xgT[:, s, k, :], start=k == 0, stop=k == CK - 1)
                    last.then_inc(e_hidden, 1)
                    pe.wait_ge(e_gated, e + 1)
                    pe.wait_ge(e_scaled, e)
                    for j in range(M_C):
                        last = nc.tensor.matmul(YB[s][:, 0, :], hid_e[:, s, j * P:(j + 1) * P], w_ed[:, s, j, :], start=j == 0, stop=j == M_C - 1)
                    last.then_inc(e_downed, 1)

        @block.scalar
        def _(act):
            act.wait_ge(consts, 8)
            for dst, src in ((before[:], d["c_before"]), (ones[:], d["c_ones"]), (count[:], d["c_count"]), (spare[:], d["c_spare"]),
                             (look[:], d["c_look"]),
                             (w_s[:, :, 0, 0:M_IS], d["L1_ffn_sw_gate"].rearrange("(k p) n -> p k n", p=P)),
                             (w_s[:, :, 1, 0:M_IS], d["L1_ffn_sw_up"].rearrange("(k p) n -> p k n", p=P)),
                             (w_sd[:, 0:M_CS - 1, :], d["L1_ffn_sw_down"][0:(M_CS - 1) * P, :].rearrange("(k p) n -> p k n", p=P)),
                             (w_sd[0:M_IS % P, M_CS - 1, :], d["L1_ffn_sw_down"][(M_CS - 1) * P:M_IS, :]),
                             (d["x3"][TOKENS:, :], zeros[:]), (d["y"][TOKENS:, :], zeros[:])):
                act.dma_start(dst, src).then_inc(loaded, 16)
            with nc.allow_non_contiguous_dma(reason="the router's weights, turned"):
                for k in range(CK):
                    act.dma_start(w_route[:, k, :], d["L1_ffn_gate_w"][:, k * P:(k + 1) * P].rearrange("e p -> p e")).then_inc(loaded, 16)
            act.wait_ge(loaded, LOADED)

            def project(b):
                act.wait_ge(o_turned, b + 1)
                for k in range(VC):
                    nc.scalar.activation(oT[:, k, :], (TB[0], TB[1], GB[0])[k][:], ACT.Copy).then_inc(oT_ready, 1)

            def body(b, ahead):
                act.wait_ge(x3_turned, b + 1)
                for k in range(CK):
                    nc.scalar.activation(x3T[:, k, :], TB[k][:], ACT.Copy).then_inc(x3T_ready, 1)
                act.wait_ge(shifted, b + 1)
                nc.scalar.activation(probs[:], probs[:], ACT.Exp).then_inc(exped, 1)
                for j in range(M_CS):
                    act.wait_ge(hidden, M_CS * b + j + 1)
                    if j == 2:
                        act.wait_ge(gated, M_CS * b + 1)
                    elif j == 0 and later(b):
                        act.wait_ge(gated, M_CS * b)
                    nc.scalar.activation(act_s[:, j % 2, :], GB[2 * (j % 2)][:], ACT.Silu).then_inc(silued, 1)
                if ahead:
                    project(b + 1)

            skewed(act, lambda: project(0), body)
            with act.Fori(0, M_E // 2) as i:
                for s in range(2):
                    e = 2 * i + s
                    act.wait_ge(xg_turned, e + 1)
                    nc.scalar.activation(xgT[:, s, :, :].rearrange("p k n -> p (k n)"), TB[s][:, 0:CK * P], ACT.Copy).then_inc(xgT_ready, 1)
                    act.wait_ge(e_hidden, e + 1)
                    nc.scalar.activation(act_e[:, s, :], GB[s][:, 0:M_C * P], ACT.Silu).then_inc(e_silued, 1)

        @block.gpsimd
        def _(pool):
            for m, value in ((mhalf, -0.5), (w_s, 0.0), (w_sd, 0.0), (w_e, 0.0), (w_ed, 0.0), (zeros, 0.0), (seen, 0.0), (scores, SENTINEL)):
                nc.gpsimd.memset(m[:], value).then_inc(consts, 1)
            nc.gpsimd.memset(chosen[:], SENTINEL).then_inc(consts, 1)
            pool.wait_ge(consts, 9)

            def normalise(b):
                pool.wait_ge(var_ready, b + 1)
                nc.gpsimd.tensor_tensor(rstd[:], rstd[:], mhalf[:], ALU.pow).then_inc(rstd_ready, 1)

            def body(b, ahead):
                pool.wait_ge(ln_done, b + 1)
                pool.sem_inc(carrier_pool)
                pool.dma_start(x3_b[b, :, :, :], x3[:]).then_inc(x3_stored, 16)
                if ahead:
                    normalise(b + 1)
                pool.wait_ge(out_ready, b + 1)
                pool.sem_inc(carrier_pool)
                pool.dma_start(y_b[b, :, :, :], y_out[:]).then_inc(y_stored, 16)

            skewed(pool, lambda: normalise(0), body)
            pool.wait_ge(x3_stored, 16 * BATCH)
            pool.wait_ge(y_stored, 16 * BATCH)
            pool.wait_ge(loaded, LOADED)

            def gather(i, s):
                e = 2 * i + s
                if later(e, 2):
                    pool.wait_ge(xg_turned, e - 1)
                pool.wait_ge(g_named, e + 1)
                if later(e, 2):
                    pool.sem_inc(carrier_pool)
                nc.gpsimd.indirect_dma_start(xg[:, s, :], None, d["x3"], bass.IndirectOffsetOnAxis(ap=g_row[:, s:s + 1], axis=0)).then_inc(gathered[s], 16)

            def scatter(e, s):
                if later(e):
                    pool.wait_ge(scattered, 16 * e)
                pool.wait_ge(e_scaled, e + 1)
                pool.sem_inc(carrier_pool)
                nc.gpsimd.indirect_dma_start(d["y"], bass.IndirectOffsetOnAxis(ap=s_row[:, s:s + 1], axis=0), out_e[:, s, :], None,
                                             compute_op=ALU.add).then_inc(scattered, 16)

            gather(0, 0)
            gather(0, 1)
            with pool.Fori(0, M_E // 2 - 1) as i:
                for s in range(2):
                    gather(i + 1, s)
                    scatter(2 * i + s, s)
            scatter(M_E - 2, 0)
            scatter(M_E - 1, 1)
            with pool.Fori(0, BATCH) as b:
                pool.wait_ge(f_var, b + 1)
                nc.gpsimd.tensor_tensor(rstd[:], rstd[:], mhalf[:], ALU.pow).then_inc(f_rstd, 1)

        @block.vector
        def _(dve):
            dve.wait_ge(loaded, LOADED)
            dve.wait_ge(consts, 9)
            made = [0, 0]

            def link(ins, b=None):
                made[0] += 1
                ins.then_inc(chain, 1)
                dve.wait_ge(chain, made[0] if b is None else ML_CHAIN * b + made[0])

            def add_x2(b):
                made[0] = 0
                dve.wait_ge(projected, b + 1)
                dve.wait_ge(x2_in, 16 * b + 16)
                for n in range(2):
                    ins = nc.vector.tensor_tensor(y[:, 2 * n:2 * n + 2, :], YB[n][:], x2[:, 2 * n:2 * n + 2, :], ALU.add)
                ins.then_inc(resid, 1)
                dve.wait_ge(resid, b + 1)
                for t in range(NT):
                    ins = nc.vector.bn_stats(stats[:, t, :], y[:, t, :])
                link(ins, b)
                dve.sem_inc(carrier_dve)
                for t in range(NT):
                    ins = nc.vector.bn_aggr(mean_var[:, t, :], stats[:, t, :])
                link(ins, b)
                nc.vector.tensor_scalar(rstd[:], mean_var[:, :, 1], EPS_LN, None, ALU.add).then_inc(var_ready, 1)

            def normalise(b):
                dve.wait_ge(rstd_ready, b + 1)
                if later(b):
                    dve.wait_ge(x3_stored, 16 * b)
                for t in range(NT):
                    ins = nc.vector.tensor_scalar(x3[:, t, :], y[:, t, :], mean_var[:, t, 0:1], rstd[:, t:t + 1], ALU.subtract, ALU.mult)
                ins.then_inc(ln_done, 1)

            def body(b, ahead):
                made[0] = 2
                vec = lambda t: t[:, :, None].broadcast_to([P, NT, M_E])
                part = lambda n: look[:].rearrange("p e (b t) s -> p b t e s", b=BATCH)[:, b, :, :, n]
                rank_b = rank[:].rearrange("p e (b t) -> p b t e", b=BATCH)[:, b, :, :]
                if later(b):
                    link(nc.vector.tensor_copy(seen[:, 0, :], seen[:, NT, :]), b)
                else:
                    link(nc.vector.tensor_copy(top[:], mhalf[:]), b)
                logits = TB[0][:, 0:NT * M_E].rearrange("p (t e) -> p t e", t=NT)
                dve.wait_ge(routed, b + 1)
                link(nc.vector.tensor_reduce(top[:], logits, AX.X, ALU.max), b)
                nc.vector.tensor_tensor(probs[:], logits, vec(top), ALU.subtract).then_inc(shifted, 1)
                dve.wait_ge(exped, b + 1)
                link(nc.vector.tensor_reduce(total[:], probs[:], AX.X, ALU.add), b)
                link(nc.vector.reciprocal(total[:], total[:]), b)
                link(nc.vector.tensor_tensor(scores[:, :, 0:M_E], probs[:], vec(total), ALU.mult), b)
                dve.sem_inc(carrier_dve)
                for t in range(NT):
                    ins = nc.vector.max(best[:, t, :], scores[:, t, 0:M_E])
                link(ins, b)
                link(nc.vector.tensor_copy(chosen[:, :, 0:M_TOP], best[:, :, 0:M_TOP]), b)
                dve.sem_inc(carrier_dve)
                for t in range(NT):
                    ins = nc.vector.match_replace(swapped[:, t, :], chosen[:, t, :], scores[:, t, :], -SENTINEL)
                link(ins, b)
                link(nc.vector.tensor_tensor(mask[:], swapped[:, :, 0:M_E], scores[:, :, 0:M_E], ALU.not_equal), b)
                for t in range(NT):
                    ins = nc.vector.tensor_tensor(seen[:, t + 1, :], seen[:, t, :], mask[:, t, :], ALU.add)
                    if t < NT - 1:
                        link(ins, b)
                ins.then_inc(masked, 1)
                link(nc.vector.tensor_reduce(total[:], best[:, :, 0:M_TOP], AX.X, ALU.add), b)
                link(nc.vector.tensor_scalar(total[:], total[:], 1e-20, None, ALU.add), b)
                link(nc.vector.reciprocal(total[:], total[:]), b)
                link(nc.vector.tensor_tensor(weight[:], scores[:, :, 0:M_E], vec(total), ALU.mult), b)
                link(nc.vector.tensor_copy(part(3), weight[:]), b)
                link(nc.vector.tensor_tensor(rest[:], weight[:], part(3), ALU.subtract), b)
                link(nc.vector.tensor_copy(part(4), rest[:]), b)
                link(nc.vector.tensor_tensor(rest[:], rest[:], part(4), ALU.subtract), b)
                link(nc.vector.tensor_copy(part(5), rest[:]), b)
                dve.wait_ge(ranked, b + 1)
                nc.vector.scalar_tensor_tensor(rank_b, TB[1][:, 0:NT * M_E].rearrange("p (t e) -> p t e", t=NT), 1.0, mask[:], ALU.add, ALU.mult)\
                    .then_inc(noted, 1)
                for j in range(M_CS):
                    dve.wait_ge(silued, M_CS * b + j + 1)
                    if j == 0 and later(b):
                        dve.wait_ge(downed, b)
                    nc.vector.tensor_tensor(hid_s[:, j, :], GB[2 * (j % 2) + 1][:], act_s[:, j % 2, :], ALU.mult).then_inc(gated, 1)
                assert made[0] == ML_CHAIN, made[0]
                if ahead:
                    add_x2(b + 1)
                dve.wait_ge(downed, b + 1)
                if later(b):
                    dve.wait_ge(y_stored, 16 * b)
                for n in range(2):
                    ins = nc.vector.tensor_tensor(y_out[:, 2 * n:2 * n + 2, :], YB[n][:], x3[:, 2 * n:2 * n + 2, :], ALU.add)
                ins.then_inc(out_ready, 1)
                if ahead:
                    dve.wait_ge(out_ready, b + 1)
                    normalise(b + 1)

            def first():
                add_x2(0)
                normalise(0)

            skewed(dve, first, body)
            dve.wait_ge(noted, BATCH)

            def take(e, s):
                if later(e, 2):
                    dve.wait_ge(looked, e - 1)
                nc.vector.tensor_tensor(onehot[:, s, :, :], count[:, None, :].broadcast_to([P, TILES, P]),
                                        rank[:, e, :, None].broadcast_to([P, TILES, P]), ALU.is_equal).then_inc(hot, 1)

            take(0, 0)
            take(1, 1)
            with dve.Fori(0, M_E // 2 - 1) as i:
                for s in range(2):
                    take(2 * i + s + 2, s)
            dve.wait_ge(looked, M_E)
            made[0] = ML_CHAIN * BATCH
            found = YB[0][:].rearrange("p a (e s) -> p (a e) s", s=8)[:, 0:M_E, :]
            nc.vector.tensor_reduce(w_slot[:, :, 0], found[:, :, 3:SLOT], AX.X, ALU.add)
            nc.vector.tensor_copy(row2[:], found[:, :, 1])
            link(nc.vector.scalar_tensor_tensor(row[:], found[:, :, 0], -1.0, spare[:], ALU.add, ALU.mult))
            link(nc.vector.tensor_tensor(row[:], row2[:], row[:], ALU.add))
            link(nc.vector.scalar_tensor_tensor(row[:], found[:, :, 2], float(P), row[:], ALU.mult, ALU.add))
            nc.vector.tensor_copy(rows[:, :, 0], row[:]).then_inc(row_ready, 1)
            dve.wait_ge(row_ready, 1)

            def name_gather(i, s):
                e = 2 * i + s
                if later(e, 2):
                    dve.wait_ge(gathered[s], 16 * i)
                nc.vector.tensor_copy(g_row[:, s:s + 1], rows[:, e, :]).then_inc(g_named, 1)

            def compute(e, s):
                dve.wait_ge(e_silued, e + 1)
                nc.vector.tensor_tensor(hid_e[:, s, :], act_e[:, s, :], GB[s][:, M_C * P:], ALU.mult).then_inc(e_gated, 1)
                dve.wait_ge(e_downed, e + 1)
                if later(e, 2):
                    dve.wait_ge(scattered, 16 * e - 16)
                nc.vector.tensor_copy(s_row[:, s:s + 1], rows[:, e, :])
                nc.vector.tensor_scalar(out_e[:, s, :], YB[s][:, 0, :], w_slot[:, e, :], None, ALU.mult).then_inc(e_scaled, 1)

            name_gather(0, 0)
            name_gather(0, 1)
            for s in range(2):
                name_gather(1, s)
                compute(s, s)
            with dve.Fori(0, M_E // 2 - 2) as i:
                for s in range(2):
                    name_gather(i + 2, s)
                    compute(2 * i + s + 2, s)
            compute(M_E - 2, 0)
            compute(M_E - 1, 1)
            with dve.Fori(0, BATCH // 2) as i:
                for s in range(2):
                    b = 2 * i + s
                    dve.wait_ge(f_in[s], 16 * i + 16)
                    for t in range(NT):
                        ins = nc.vector.bn_stats(stats[:, t, :], y_in[:, s, t, :])
                    ins.then_inc(f_chain, 1)
                    dve.wait_ge(f_chain, 2 * b + 1)
                    dve.sem_inc(carrier_dve)
                    for t in range(NT):
                        ins = nc.vector.bn_aggr(mean_var[:, t, :], stats[:, t, :])
                    ins.then_inc(f_chain, 1)
                    dve.wait_ge(f_chain, 2 * b + 2)
                    nc.vector.tensor_scalar(rstd[:], mean_var[:, :, 1], EPS_LN, None, ALU.add).then_inc(f_var, 1)
                    dve.wait_ge(f_rstd, b + 1)
                    dve.wait_ge(f_stored[s], 16 * i)
                    for t in range(NT):
                        ins = nc.vector.tensor_scalar(final[:, s, t, :], y_in[:, s, t, :], mean_var[:, t, 0:1], rstd[:, t:t + 1], ALU.subtract, ALU.mult)
                    ins.then_inc(f_done, 1)
                    dve.wait_ge(f_done, b + 1)
    nc.clear_and_free_semaphores(sems)
    nc.all_engine_barrier()


def whole_program(nc, d, out):
    d = dict(d)
    n_tok, blocks = TOKENS, (NB, TILES, BLK, BLK)
    for name, shape in (("x1", (n_tok, C)), ("x2", (n_tok, C)), ("gate", (n_tok, VDIM)), ("v", (n_tok, VDIM)), ("o", (n_tok, VDIM)),
                        ("hT", (P, CK, n_tok)), ("beta", (P, D_H, TILES)), ("g", (P, D_H, TILES)), ("decays", (P, 3, D_H, TILES)),
                        ("a_blk", blocks), ("u_blk", blocks), ("l_blk", blocks), ("x3", (n_tok + CAP, C)), ("y", (n_tok + CAP, C))):
        d[name] = nc.dram_tensor("mid_" + name, shape, F32).ap()
    d["out"] = out.rearrange("b t c -> (b t) c")
    layer0_attention(nc, d)
    layer0_experts(nc, d)
    layer1_projections(nc, d)
    layer1_delta_rule(nc, d)
    layer1_output(nc, d)


def kernel(**inputs):
    import concourse.bacc as bacc
    from concourse.bass_utils import run_bass_kernel_spmd

    nc = bacc.Bacc("TRN2", target_bir_lowering=False, num_devices=1)
    arrays = {name: np.ascontiguousarray(a) for name, a in inputs.items()}
    arrays.update(constants())
    arrays.update(delta_constants())
    arrays.update(expert_constants())
    d = {name: nc.dram_tensor(name, a.shape, mybir.dt.from_np(a.dtype), kind="ExternalInput").ap() for name, a in arrays.items()}
    out = nc.dram_tensor("out", (BATCH, T, C), F32, kind="ExternalOutput").ap()
    whole_program(nc, d, out)
    result = run_bass_kernel_spmd(nc, [arrays], core_ids=[0])
    return result.results[0]["out"]
```
